# Optimizing a Trainium2 kernel written in Bass

```python
import numpy as np
import jax
import jax.numpy as jnp

def _softmax(x, axis=-1):
    return jax.nn.softmax(x, axis=axis)

def _gelu(x):
    return jax.nn.gelu(x, approximate=True)

def _silu(x):
    return jax.nn.silu(x)

def _sigmoid(x):
    return jax.nn.sigmoid(x)

def _layernorm(x, axis=-1, eps=1e-05):
    m = jnp.mean(x, axis=axis, keepdims=True)
    v = jnp.var(x, axis=axis, keepdims=True)
    return (x - m) / jnp.sqrt(v + eps)

def _scatter_add(tgt, idx, src, axis=0):
    return tgt.at[idx].add(src)

def _segment_sum(src, seg, n):
    return jax.ops.segment_sum(src, seg, n)
kernel_name = 'mk_rec_standalone_d1_rec_r8_9c95ec'

def setup_inputs(seed: int=0):
    np.random.seed(seed)
    _w = jnp.asarray

    def _rec_inputs():
        import jax
        import jax.numpy as jnp
        _rk = jax.random.key(seed)
        r_keys = -0.0002422 + 0.999987 * jax.random.normal(jax.random.fold_in(_rk, 1), (2048, 200, 64), jnp.float32)
        r_queries = -0.00356592 + 0.997978 * jax.random.normal(jax.random.fold_in(_rk, 2), (2048, 1, 64), jnp.float32)
        r_mask = jax.random.randint(jax.random.fold_in(_rk, 3), (2048, 200), 0, 2, jnp.int32)
        return (r_keys, r_queries, r_mask)
    r_keys, r_queries, r_mask = _rec_inputs()

    def _L0_rec_setup():
        import jax, jax.numpy as jnp
        import numpy as np
        EPS = 1e-08

        def dice(x, alpha, gamma, beta):
            mean = jnp.mean(x, axis=(0, 1))
            var = jnp.var(x, axis=(0, 1))
            xn = (x - mean) * jax.lax.rsqrt(var + EPS) * gamma + beta
            p = jax.nn.sigmoid(xn)
            return p * x + (1.0 - p) * alpha * x
        key = jax.random.key(seed)
        ks = jax.random.split(key, 8)
        B, L, E = (256, 200, 64)
        H1, H2 = (80, 40)
        inp = {'keys': jax.random.normal(ks[0], (B, L, E), dtype=jnp.float32), 'queries': jax.random.normal(ks[1], (B, 1, E), dtype=jnp.float32), 'mask': jax.random.randint(ks[2], (B, L), 0, 2, dtype=jnp.int32), 'W1': jax.random.normal(ks[3], (4 * E, H1), dtype=jnp.float32) / np.sqrt(4 * E), 'b1': jnp.zeros((H1,), dtype=jnp.float32), 'alpha1': jnp.zeros((H1,), dtype=jnp.float32), 'g1': jnp.ones((H1,), dtype=jnp.float32), 'be1': jnp.zeros((H1,), dtype=jnp.float32), 'W2': jax.random.normal(ks[4], (H1, H2), dtype=jnp.float32) / np.sqrt(H1), 'b2': jnp.zeros((H2,), dtype=jnp.float32), 'alpha2': jnp.zeros((H2,), dtype=jnp.float32), 'g2': jnp.ones((H2,), dtype=jnp.float32), 'be2': jnp.zeros((H2,), dtype=jnp.float32), 'W3': jax.random.normal(ks[5], (H2, 1), dtype=jnp.float32) / np.sqrt(H2), 'b3': jnp.zeros((1,), dtype=jnp.float32), 'alpha3': jnp.zeros((1,), dtype=jnp.float32), 'g3': jnp.ones((1,), dtype=jnp.float32), 'be3': jnp.zeros((1,), dtype=jnp.float32)}
        return inp
    _L0_rec_all = _L0_rec_setup()
    _L0_rec_in = {k: v for k, v in _L0_rec_all.items() if k in ('W1', 'b1', 'alpha1', 'g1', 'be1', 'W2', 'b2', 'alpha2', 'g2', 'be2', 'W3', 'b3', 'alpha3', 'g3', 'be3')}
    del _L0_rec_all
    return {'r_keys': r_keys, 'r_queries': r_queries, 'r_mask': r_mask, 'L0_rec_W1': _L0_rec_in['W1'], 'L0_rec_b1': _L0_rec_in['b1'], 'L0_rec_alpha1': _L0_rec_in['alpha1'], 'L0_rec_g1': _L0_rec_in['g1'], 'L0_rec_be1': _L0_rec_in['be1'], 'L0_rec_W2': _L0_rec_in['W2'], 'L0_rec_b2': _L0_rec_in['b2'], 'L0_rec_alpha2': _L0_rec_in['alpha2'], 'L0_rec_g2': _L0_rec_in['g2'], 'L0_rec_be2': _L0_rec_in['be2'], 'L0_rec_W3': _L0_rec_in['W3'], 'L0_rec_b3': _L0_rec_in['b3'], 'L0_rec_alpha3': _L0_rec_in['alpha3'], 'L0_rec_g3': _L0_rec_in['g3'], 'L0_rec_be3': _L0_rec_in['be3']}

def reference(r_keys, r_queries, r_mask, L0_rec_W1, L0_rec_b1, L0_rec_alpha1, L0_rec_g1, L0_rec_be1, L0_rec_W2, L0_rec_b2, L0_rec_alpha2, L0_rec_g2, L0_rec_be2, L0_rec_W3, L0_rec_b3, L0_rec_alpha3, L0_rec_g3, L0_rec_be3):
    import jax
    import jax.numpy as jnp

    def _L0_rec_ref(keys, queries, mask, W1, b1, alpha1, g1, be1, W2, b2, alpha2, g2, be2, W3, b3, alpha3, g3, be3):
        import jax, jax.numpy as jnp
        import numpy as np
        EPS = 1e-08

        def dice(x, alpha, gamma, beta):
            mean = jnp.mean(x, axis=(0, 1))
            var = jnp.var(x, axis=(0, 1))
            xn = (x - mean) * jax.lax.rsqrt(var + EPS) * gamma + beta
            p = jax.nn.sigmoid(xn)
            return p * x + (1.0 - p) * alpha * x
        B, L, E = keys.shape
        q = jnp.broadcast_to(queries, (B, L, E))
        att_in = jnp.concatenate([q, keys, q - keys, q * keys], axis=-1)
        h = dice(att_in @ W1 + b1, alpha1, g1, be1)
        h = dice(h @ W2 + b2, alpha2, g2, be2)
        s = dice(h @ W3 + b3, alpha3, g3, be3)
        score = jnp.swapaxes(s, 1, 2)
        m = (1 - mask)[:, None, :].astype(score.dtype)
        out = jnp.matmul(score * m, keys)
        return out
    y = _L0_rec_ref(r_keys, r_queries, r_mask, L0_rec_W1, L0_rec_b1, L0_rec_alpha1, L0_rec_g1, L0_rec_be1, L0_rec_W2, L0_rec_b2, L0_rec_alpha2, L0_rec_g2, L0_rec_be2, L0_rec_W3, L0_rec_b3, L0_rec_alpha3, L0_rec_g3, L0_rec_be3)
    return y

_drawn_inputs = setup_inputs


def setup_inputs(seed=0):
    import zlib

    import numpy as np

    out = dict(_drawn_inputs(seed))
    spreads = {'L0_rec_b1': (0.0, 0.1),
     'L0_rec_alpha1': (0.0, 0.1),
     'L0_rec_g1': (1.0, 0.2),
     'L0_rec_be1': (0.0, 0.1),
     'L0_rec_b2': (0.0, 0.1),
     'L0_rec_alpha2': (0.0, 0.1),
     'L0_rec_g2': (1.0, 0.2),
     'L0_rec_be2': (0.0, 0.372)}
    factors = {}
    for name, (base, spread) in spreads.items():
        noise = np.random.default_rng([zlib.crc32(name.encode()), seed]).standard_normal(out[name].shape)
        drawn = base * np.exp(spread * noise) if base else spread * noise
        out[name] = jnp.asarray(drawn.astype(out[name].dtype))
    for name, factor in factors.items():
        out[name] = (out[name] * factor).astype(out[name].dtype)
    return out
```

```python
from contextlib import ExitStack

import concourse.bass as bass
from concourse import mybir

F32 = mybir.dt.float32
I32 = mybir.dt.int32
ALU = mybir.AluOpType
ACT = mybir.ActivationFunctionType

P = 128
BATCHES, TOKENS, E = 2048, 200, 64
H1, H2 = 80, 40
EPS = 1e-8
TINY = 2.0 ** -40
BANK = 512

GROUPS = BATCHES // 8
COLS = 4 * TOKENS
RING = 4
BLOCKS = GROUPS // RING
MAIN = 64
REST = H1 - MAIN
MCOLS = MAIN + 2 * REST

TILES_C = GROUPS // 2
FULL = 16
FULLS = TILES_C // FULL
RING_C = 4

UNITS = BATCHES // 32
RING_D = 4
CHUNKS = (96, 104)
CH = max(CHUNKS)

K_ID = 0
K_GA = K_ID + P
K_GB = K_GA + P
K_SA = K_GB + P
K_SB = K_SA + H1
K_G2 = K_SB + H1
K_S2 = K_G2 + P
K_G3 = K_S2 + 2 * H2
K_COLS = K_G3 + P

(Q_B1A, Q_B1B, Q_G1, Q_BE1, Q_AL1, Q_B2, Q_G2, Q_BE2, Q_AL2, Q_W3A, Q_W3B, Q_B3, Q_G3, Q_BE3,
 Q_AL3, Q_W2) = range(16)
Q_COLS = Q_W2 + H2


def mask_dice_attention(nc, keysT, keysU, queriesT, mask, w1, params, consts, x1_main, x1_rest, x2_dram, out):
    with ExitStack() as ctx:
        def sb(name, shape, dt=F32):
            return ctx.enter_context(nc.sbuf_tensor(name, shape, dt))

        def sem(name):
            return ctx.enter_context(nc.semaphore(name))

        def sems(name, n):
            return [sem(f"{name}{r}") for r in range(n)]

        psum = ctx.enter_context(nc.psum_tensor("psum", [P, 8, BANK], F32))

        con = sb("con", [P, K_COLS])
        par = sb("par", [P, Q_COLS])
        w1s = sb("w1s", [P, 4, H1])
        wA = sb("wA", [P, H1])
        wArest = sb("wArest", [P, 2 * REST])
        wB = sb("wB", [P, MCOLS])
        wD = sb("wD", [P, MCOLS])
        tmp = sb("tmp", [P, 16])
        w2d = sb("w2d", [P, 64])
        w2a = sb("w2a", [P, 64])
        w3z = sb("w3z", [P, 62])
        sc1 = sb("sc1", [P, 4])
        sc2 = sb("sc2", [P, 4])
        sc3 = sb("sc3", [P, 4])

        n_ad = max(RING * (COLS + 4 * MCOLS + COLS) + 2 * 2 * TOKENS + 2 * (GROUPS * 4) + GROUPS
                   + 6 * (2 * GROUPS + GROUPS // 2),
                   RING_D * 2 * 4 * BANK + 2 * (BATCHES + 32) + RING_D * 2 * 64 + 2 * RING_D * BANK)
        n_bc = max(RING * (2 * 2 * COLS + COLS) + 12 * GROUPS,
                   2 * RING_C * 2 * COLS + 3 * FULLS * 2 * TOKENS)
        arena_ad = sb("arena_ad", [P, n_ad])
        arena_bc = sb("arena_bc", [P, n_bc])

        def cutter(arena):
            at = [0]

            def cut(n):
                at[0] += n
                return arena[:, at[0] - n:at[0]]
            return cut

        cut = cutter(arena_ad)
        keysA = cut(RING * COLS).rearrange("p (r n) -> p r n", r=RING)
        wM = cut(RING * 4 * MCOLS).rearrange("p (r j m) -> p r j m", r=RING, j=4)
        xMain = cut(RING * COLS).rearrange("p (r n) -> p r n", r=RING)
        xRest = cut(2 * 2 * TOKENS).rearrange("p (r n) -> p r n", r=2)
        qT = cut(GROUPS * 4)
        cMain = cut(GROUPS * 4)
        cRest = cut(GROUPS)
        stMain = cut(6 * 2 * GROUPS)
        stRest = cut(6 * GROUPS // 2)

        cut = cutter(arena_ad)
        keysD = cut(RING_D * 2 * 4 * BANK).rearrange("p (r c t n) -> p r c t n", r=RING_D, c=2, t=4)
        sT = cut(2 * (BATCHES + 32)).rearrange("p (c n) -> p c n", c=2)
        sU = cut(RING_D * 2 * 64).rearrange("p (r c n) -> p r c n", r=RING_D, c=2)
        oD = cut(2 * RING_D * BANK).rearrange("p (s u n) -> p s u n", s=2, u=RING_D)

        cut = cutter(arena_bc)
        x1 = cut(RING * 2 * COLS).rearrange("p (r n) -> p r n", r=RING)
        h1 = cut(RING * 2 * COLS).rearrange("p (r n) -> p r n", r=RING)
        x2 = cut(RING * COLS).rearrange("p (r n) -> p r n", r=RING)
        st2 = cut(12 * GROUPS)

        cut = cutter(arena_bc)
        x2c = cut(RING_C * 2 * COLS).rearrange("p (r g n) -> p r g n", r=RING_C, g=2)
        x3 = cut(FULLS * 2 * TOKENS)
        s3 = cut(FULLS * 2 * TOKENS)
        maskI = cut(FULLS * 2 * TOKENS).bitcast(I32)
        p2 = cut(RING_C * 2 * COLS).rearrange("p (r n) -> p r n", r=RING_C)
        st3 = sb("st3", [P, 6 * FULLS])

        const_loaded = sem("const_loaded")
        keysA_loaded = sems("keysA_loaded", RING)
        x1main_stored = sems("x1main_stored", RING)
        x1rest_stored = sems("x1rest_stored", 2)
        x1_loaded = sems("x1_loaded", RING)
        x2_stored = sems("x2_stored", RING)
        x2c_loaded = sems("x2c_loaded", RING_C)
        mask_loaded = sem("mask_loaded")
        keysD_loaded = sems("keysD_loaded", RING_D)
        out_stored = sems("out_stored", 2)
        small = sem("small")
        setup_done = sem("setup_done")
        c_ready = sem("c_ready")
        wM_built = sems("wM_built", RING)
        wM_scaled = sem("wM_scaled")
        x1_done = sems("x1_done", RING)
        main_out = sems("main_out", 2)
        rest_out = sems("rest_out", 2)
        st_main_done = sems("st_main_done", RING)
        st_rest_done = sems("st_rest_done", 2)
        stat_in = sem("stat_in")
        stat_sum = sem("stat_sum")
        root_in = sem("root_in")
        root_out = sem("root_out")
        dice_ready = sem("dice_ready")
        p1_ready = sems("p1_ready", RING)
        h1_ready = sems("h1_ready", RING)
        y1_ready = sems("y1_ready", RING)
        x2_done = sems("x2_done", RING)
        x2_out = sems("x2_out", RING)
        st2_done = sems("st2_done", RING)
        p2_ready = sems("p2_ready", RING_C)
        h2_ready = sems("h2_ready", RING_C)
        x3_done = sems("x3_done", RING_C)
        x3_out = sem("x3_out")
        p3_ready = sem("p3_ready")
        s_ready = sem("s_ready")
        sT_done = sem("sT_done")
        sT_out = sem("sT_out")
        sU_ready = sems("sU_ready", RING_D)
        o_done = sems("o_done", RING_D)
        o_out = sems("o_out", RING_D)

        block = ctx.enter_context(nc.Block())

        @block.sync
        def _(sp):
            sp.dma_start(con[:, :], consts).then_inc(const_loaded, 16)
            sp.dma_start(par[:, :], params).then_inc(const_loaded, 16)
            w1_v = w1.rearrange("(i e) c -> e i c", i=4)
            for h in range(2):
                sp.dma_start(w1s[64 * h:64 * h + 64, :, :], w1_v).then_inc(const_loaded, 16)
            sp.dma_start(qT, queriesT).then_inc(const_loaded, 16)

            def load_keys(i, r):
                sp.dma_start(keysA[:, r, :], keysT[bass.ds(RING * i + r, 1), :, :]
                             .rearrange("a p n -> (a p) n")).then_inc(keysA_loaded[r], 16)

            def store_x1(i, r):
                sp.wait_ge(main_out[r % 2], 2 * i + (r // 2 + 1))
                sp.dma_start(x1_main[bass.ds(RING * i + r, 1), :, :].rearrange("a p n -> (a p) n"),
                             xMain[:, r, :]).then_inc(x1main_stored[r], 16)
                if r % 2:
                    b = r // 2
                    sp.wait_ge(rest_out[b], i + 1)
                    sp.dma_start(x1_rest[bass.ds(2 * i + b, 1), :, :].rearrange("a p n -> (a p) n"),
                                 xRest[:, b, :]).then_inc(x1rest_stored[b], 16)

            for r in range(RING):
                load_keys(0, r)
            with sp.Fori(1, BLOCKS) as i:
                for r in range(RING):
                    sp.wait_ge(x1_done[r], i)
                    load_keys(i, r)
                    store_x1(i - 1, r)
            for r in range(RING):
                store_x1(BLOCKS - 1, r)

            for r in range(RING):
                sp.wait_ge(x1main_stored[r], 16 * BLOCKS)
            for b in range(2):
                sp.wait_ge(x1rest_stored[b], 16 * BLOCKS)

            def load_x1(i, r):
                sp.dma_start(x1[0:MAIN, r, :].rearrange("c (h n) -> c h n", h=2),
                             x1_main[bass.ds(RING * i + r, 1), :, :]
                             .rearrange("a (h c) n -> (a c) h n", h=2)).then_inc(x1_loaded[r], 16)
                g = r % 2
                rest = x1_rest[bass.ds(2 * i + r // 2, 1), :, g * TOKENS:(g + 1) * TOKENS]
                for h in range(2):
                    sp.dma_start(x1[MAIN:H1, r, h * COLS:(h + 1) * COLS].rearrange("c (j t) -> c j t", j=4),
                                 rest.rearrange("a (j h c) t -> h (a c) j t", j=4, h=2)[h]
                                 ).then_inc(x1_loaded[r], 16)

            def store_x2(i, r):
                sp.wait_ge(x2_out[r], i + 1)
                for h in range(2):
                    sp.dma_start(x2_dram[bass.ds(RING * i + r, 1), h * H2:(h + 1) * H2, :]
                                 .rearrange("a c n -> (a c) n"),
                                 x2[64 * h:64 * h + H2, r, :]).then_inc(x2_stored[r], 16)

            for r in range(RING):
                load_x1(0, r)
            with sp.Fori(1, BLOCKS) as i:
                for r in range(RING):
                    sp.wait_ge(x2_done[r], i)
                    load_x1(i, r)
                    store_x2(i - 1, r)
            for r in range(RING):
                store_x2(BLOCKS - 1, r)

            for r in range(RING):
                sp.wait_ge(x2_stored[r], 32 * BLOCKS)
                sp.wait_ge(st2_done[r], BLOCKS)
            sp.dma_start(maskI, mask).then_inc(mask_loaded, 16)

            def load_x2(F, t):
                sp.dma_start(x2c[0:2 * H2, t % RING_C, :, :],
                             x2_dram[bass.ds(2 * (FULL * F + t), 2), :, :].rearrange("g c n -> c g n")
                             ).then_inc(x2c_loaded[t % RING_C], 16)

            def load_unit(i, r):
                for c, n in enumerate(CHUNKS):
                    sp.dma_start(keysD[0:n, r, c, :, :],
                                 keysU[bass.ds(RING_D * i + r, 1), c * CHUNKS[0]:c * CHUNKS[0] + n, :, :]
                                 .rearrange("a p t n -> (a p) t n")).then_inc(keysD_loaded[r], 16)

            for t in range(RING_C):
                load_x2(0, t)
            for r in range(RING_D):
                load_unit(0, r)
            for t in range(RING_C, FULL):
                sp.wait_ge(x3_done[t % RING_C], t // RING_C)
                load_x2(0, t)
            with sp.Fori(1, FULLS) as F:
                for t in range(FULL):
                    sp.wait_ge(x3_done[t % RING_C], (FULL // RING_C) * F + t // RING_C)
                    load_x2(F, t)

            def store_out(i, s):
                for b in range(8):
                    sp.dma_start(out[bass.ds(RING_D * i, RING_D), :, b, :].rearrange("u t e -> t u e"),
                                 oD[b:b + 97:32, s, :, E * b:E * b + E]).then_inc(out_stored[s], 16)

            def blocks_d(i, s):
                for r in range(RING_D):
                    sp.wait_ge(o_done[r], i)
                    load_unit(i, r)
                for r in range(RING_D):
                    sp.wait_ge(o_out[r], i)
                store_out(i - 1, s)

            n_d = UNITS // RING_D
            with sp.Fori(0, n_d // 2 - 1) as i2:
                blocks_d(2 * i2 + 1, 0)
                blocks_d(2 * i2 + 2, 1)
            blocks_d(n_d - 1, 0)
            for r in range(RING_D):
                sp.wait_ge(o_out[r], n_d)
            store_out(n_d - 1, 1)
            for s in range(2):
                sp.wait_ge(out_stored[s], 16 * 8 * (n_d // 2))

        @block.gpsimd
        def _(pool):
            pool.wait_ge(setup_done, 1)
            with pool.Fori(0, BLOCKS) as i:
                for r in range(RING):
                    pool.wait_ge(x1_done[r], i)
                    q = qT[:, bass.ds(4 * RING * i + 4 * r, 4)]
                    pool.tensor_tensor(wM[:, r, :, :], q.unsqueeze(2).broadcast_to([P, 4, MCOLS]),
                                       wD[:, :].unsqueeze(1).broadcast_to([P, 4, MCOLS]),
                                       ALU.mult).then_inc(wM_scaled, 1)
                    pool.wait_ge(wM_scaled, RING * i + (r + 1))
                    pool.tensor_tensor(wM[:, r, :, :], wM[:, r, :, :],
                                       wB[:, :].unsqueeze(1).broadcast_to([P, 4, MCOLS]),
                                       ALU.add).then_inc(wM_built[r], 1)

            c0 = 2 * COLS - COLS // 2
            with pool.Fori(0, BLOCKS) as i:
                for r in range(RING):
                    pool.wait_ge(p1_ready[r], i + 1)
                    pool.tensor_tensor(h1[0:H1, r, c0:], h1[0:H1, r, c0:], x1[0:H1, r, c0:],
                                       ALU.mult).then_inc(y1_ready[r], 1)

        @block.tensor
        def _(pe):
            pe.wait_ge(setup_done, 1)
            half = GROUPS * 2
            for n in range(2):
                for h in range(2):
                    rows = slice(64 * h, 64 * h + 64)
                    pe.matmul(psum[rows, n, 0:half], wA[rows, 0:MAIN], qT[rows, n * half:(n + 1) * half],
                              start=True, stop=True)
            qj = qT.rearrange("p (g j) -> p j g", j=4)
            for j in range(4):
                last = pe.matmul(psum[32 * j:32 * j + 32, 2, 0:GROUPS], wArest[:, :], qj[:, j, :],
                                 start=True, stop=True)
            last.then_inc(c_ready, 1)
            pe.wait_ge(small, SMALL_C)

            with pe.Fori(0, BLOCKS) as i:
                for r in range(RING):
                    s, b = r % 2, r // 2
                    pe.wait_ge(keysA_loaded[r], 16 * i + 16)
                    pe.wait_ge(wM_built[r], i + 1)
                    pe.wait_ge(main_out[s], 2 * i + r // 2)
                    if s == 0:
                        pe.wait_ge(rest_out[b], i)
                    for j in range(4):
                        pe.matmul(psum[32 * j:32 * j + 32, 4 + b, s * TOKENS:(s + 1) * TOKENS],
                                  wM[:, r, j, MAIN:MCOLS], keysA[:, r, j * TOKENS:(j + 1) * TOKENS],
                                  start=True, stop=True)
                    for j in range(4):
                        c = (j % 2) * TOKENS
                        for h in range(2):
                            rows = slice(64 * h, 64 * h + 64)
                            last = pe.matmul(psum[rows, 2 * s + j // 2, c:c + TOKENS], wM[rows, r, j, 0:MAIN],
                                      keysA[rows, r, j * TOKENS:(j + 1) * TOKENS], start=True, stop=True)
                    last.then_inc(x1_done[r], 1)

            def averages(step, outs):
                pe.wait_ge(stat_in, step)
                for col, terms in outs:
                    for n, (k, m, v) in enumerate(terms):
                        last = pe.matmul(psum[0:m, 6, col:col + 1], con[:, k:k + m], tmp[:, v:v + 1],
                                         start=(n == 0), stop=(n == len(terms) - 1))
                last.then_inc(stat_sum, 1)

            averages(1, [(0, [(K_GA, P, 0)]), (3, [(K_GB, P, 2)])])
            averages(2, [(1, [(K_SA, H1, 0), (K_SB, H1, 2)]), (2, [(K_SA, H1, 4), (K_SB, H1, 6)])])

            pe.wait_ge(dice_ready, 1)
            with pe.Fori(0, BLOCKS) as i:
                for r in range(RING):
                    pe.wait_ge(x2_out[r], i)
                    pe.wait_ge(h1_ready[r], i + 1)
                    for a in range(2):
                        for h in range(2):
                            c = h * COLS + a * (COLS // 2)
                            whole = (a, h) != (1, 1)
                            if not whole:
                                pe.wait_ge(y1_ready[r], i + 1)
                            last = pe.matmul(psum[64 * h:64 * h + 64, 2 * r + a, 0:COLS // 2], w2d[0:H1, :],
                                             h1[0:H1, r, c:c + COLS // 2], start=True, stop=whole)
                    last = pe.matmul(psum[64:P, 2 * r + 1, 0:COLS // 2], w2a[0:H1, :],
                                     x1[0:H1, r, c:c + COLS // 2], start=False, stop=True)
                    last.then_inc(x2_done[r], 1)

            averages(3, [(0, [(K_G2, P, 0)])])
            averages(4, [(1, [(K_S2, 2 * H2, 0)]), (2, [(K_S2, 2 * H2, 4)])])

            pe.wait_ge(dice_ready, 2)
            with pe.Fori(0, FULLS) as F:
                pe.wait_ge(x3_out, F)
                for t in range(FULL):
                    q = t % RING_C
                    pe.wait_ge(h2_ready[q], (FULL // RING_C) * F + (t // RING_C + 1))
                    for g in range(2):
                        for a in range(2):
                            ct = 2 * g + a
                            last = pe.matmul(psum[32 * ct:32 * ct + 32, 0, 0:2 * TOKENS],
                                             w3z[0:2 * H2, 30 - 2 * t:62 - 2 * t],
                                             p2[0:2 * H2, q, g * COLS + a * 2 * TOKENS:
                                                g * COLS + (a + 1) * 2 * TOKENS],
                                             start=(t == 0), stop=(t == FULL - 1))
                    last.then_inc(x3_done[q], 1)

            averages(5, [(0, [(K_G3, P, 0)])])
            averages(6, [(1, [(K_G3, P, 4)])])

            pe.wait_ge(s_ready, 1)
            for n in range(2 * FULLS):
                c0 = 0
                if n >= 2:
                    pe.wait_ge(sT_out, 2 * n - 1)
                for c, m in enumerate(CHUNKS):
                    last = pe.transpose(psum[0:m, 2 + n % 2, c * P:(c + 1) * P],
                                        s3[:, n * TOKENS + c0:n * TOKENS + c0 + m], con[:, K_ID:K_ID + P])
                    c0 += m
                last.then_inc(sT_done, 1)

            with pe.Fori(0, UNITS // RING_D) as i:
                for r in range(RING_D):
                    pe.wait_ge(keysD_loaded[r], 32 * i + 32)
                    pe.wait_ge(sU_ready[r], i + 1)
                    pe.wait_ge(o_out[r], i)
                    for c, n in enumerate(CHUNKS):
                        for t in range(4):
                            last = pe.matmul(psum[32 * t:32 * t + 32, 4 + r, :], sU[0:n, r, c, 8 * t:8 * t + 32],
                                             keysD[0:n, r, c, t, :], start=(c == 0), stop=(c == 1))
                    last.then_inc(o_done[r], 1)

        @block.scalar
        def _(act):
            def root(n):
                act.wait_ge(root_in, n)
                act.activation(tmp[:, 9:10], tmp[:, 8:9], ACT.Sqrt).then_inc(root_out, 1)

            root(1)

            act.wait_ge(dice_ready, 1)

            def sigmoid1(i, r):
                act.wait_ge(x1_loaded[r], 48 * i + 48)
                act.wait_ge(x2_done[r], i)
                act.activation(h1[0:H1, r, :], x1[0:H1, r, :], ACT.Sigmoid, bias=sc1[0:H1, 1:2],
                               scale=sc1[0:H1, 0:1]).then_inc(p1_ready[r], 1)

            def x2_from_psum(i, r):
                act.wait_ge(x2_done[r], i + 1)
                act.wait_ge(x2_stored[r], 32 * i)
                act.wait_ge(st2_done[r], i)
                act.activation(x2[:, r, :].rearrange("p (a n) -> p a n", a=2),
                               psum[:, 2 * r:2 * r + 2, 0:COLS // 2], ACT.Identity,
                               bias=par[:, Q_B2:Q_B2 + 1]).then_inc(x2_out[r], 1)

            for r in range(RING):
                sigmoid1(0, r)
                if r >= 2:
                    x2_from_psum(0, r - 2)
            with act.Fori(1, BLOCKS) as i:
                for r in range(RING):
                    sigmoid1(i, r)
                    x2_from_psum(i if r >= 2 else i - 1, (r - 2) % RING)
            for r in (2, 3):
                x2_from_psum(BLOCKS - 1, r)

            root(2)

            act.wait_ge(dice_ready, 2)
            with act.Fori(0, FULLS) as F:
                for t in range(FULL):
                    q = t % RING_C
                    act.wait_ge(x2c_loaded[q], 16 * ((FULL // RING_C) * F + (t // RING_C + 1)))
                    act.wait_ge(x3_done[q], (FULL // RING_C) * F + t // RING_C)
                    act.activation(p2[0:2 * H2, q, :], x2c[0:2 * H2, q, :, :].rearrange("p g n -> p (g n)"),
                                   ACT.Sigmoid, bias=sc2[0:2 * H2, 1:2], scale=sc2[0:2 * H2, 0:1]
                                   ).then_inc(p2_ready[q], 1)

            root(3)
            act.wait_ge(dice_ready, 3)
            act.activation(s3, x3, ACT.Sigmoid, bias=sc3[:, 1:2], scale=sc3[:, 0:1]).then_inc(p3_ready, 1)

            act.wait_ge(sT_out, 4 * FULLS + 1)
            with act.Fori(0, UNITS // RING_D) as i:
                for r in range(RING_D):
                    act.wait_ge(o_done[r], i)
                    for c, n in enumerate(CHUNKS):
                        last = act.copy(sU[0:n, r, c, 0:56], sT[0:n, c, bass.ds(32 * (RING_D * i + r), 56)])
                    last.then_inc(sU_ready[r], 1)

        @block.vector
        def _(v):
            steps = [0]

            def link(ins):
                steps[0] += 1
                ins.then_inc(small, 1)
                v.wait_ge(small, steps[0])

            def col(k, rows=P):
                return tmp[0:rows, k:k + 1]

            v.wait_ge(const_loaded, 80)
            link(v.memset(wB[:, MAIN:MCOLS], 0.0))
            link(v.memset(wD[:, MAIN:MCOLS], 0.0))
            link(v.memset(wArest[:, :], 0.0))
            link(v.memset(w2d[:, :], 0.0))
            link(v.memset(w2a[:, :], 0.0))
            link(v.memset(w3z[:, :], 0.0))
            link(v.memset(tmp[:, :], 0.0))
            link(v.tensor_tensor(wA[:, :], w1s[:, 0, :], w1s[:, 2, :], ALU.add))
            link(v.tensor_tensor(wB[:, 0:MAIN], w1s[:, 1, 0:MAIN], w1s[:, 2, 0:MAIN], ALU.subtract))
            link(v.tensor_copy(wD[:, 0:MAIN], w1s[:, 3, 0:MAIN]))
            for h in range(2):
                rows, at = slice(64 * h, 64 * h + 64), REST * h
                link(v.tensor_copy(wArest[rows, at:at + REST], wA[rows, MAIN:H1]))
                link(v.tensor_tensor(wB[rows, MAIN + at:MAIN + at + REST], w1s[rows, 1, MAIN:H1],
                                     w1s[rows, 2, MAIN:H1], ALU.subtract))
                link(v.tensor_copy(wD[rows, MAIN + at:MAIN + at + REST], w1s[rows, 3, MAIN:H1]))
            v.memset(tmp[:, 15:16], 0.0).then_inc(setup_done, 1)

            v.wait_ge(c_ready, 1)
            link(v.tensor_scalar(cMain.rearrange("p (a n) -> p a n", a=2), psum[:, 0:2, 0:2 * GROUPS],
                                 par[:, Q_B1A:Q_B1A + 1], None, ALU.add))
            link(v.tensor_scalar(cRest, psum[:, 2, 0:GROUPS], par[:, Q_B1B:Q_B1B + 1], None, ALU.add))
            assert steps[0] == SMALL_C

            def stats_main(i, r):
                v.wait_ge(main_out[r % 2], 2 * i + (r // 2 + 1))
                for a in range(2):
                    last = v.bn_stats(stMain[:, bass.ds(12 * (RING * i + r) + 6 * a, 6)],
                                      xMain[:, r, a * 2 * TOKENS:(a + 1) * 2 * TOKENS])
                last.then_inc(st_main_done[r], 1)

            with v.Fori(0, BLOCKS) as i:
                for r in range(RING):
                    s, b = r % 2, r // 2
                    v.wait_ge(x1_done[r], i + 1)
                    v.wait_ge(x1main_stored[r], 16 * i)
                    v.wait_ge(st_main_done[r], i)
                    c = cMain[:, bass.ds(4 * (RING * i + r), 4)].rearrange("p (a j) -> p a j", a=2)
                    v.tensor_tensor(xMain[:, r, :].rearrange("p (a j t) -> p a j t", a=2, j=2),
                                    psum[:, 2 * s:2 * s + 2, 0:2 * TOKENS].rearrange("p a (j t) -> p a j t", j=2),
                                    c.unsqueeze(3).broadcast_to([P, 2, 2, TOKENS]),
                                    ALU.add).then_inc(main_out[s], 1)
                    if s == 1:
                        v.wait_ge(x1rest_stored[b], 16 * i)
                        v.wait_ge(st_rest_done[b], i)
                        c = cRest[:, bass.ds(RING * i + 2 * b, 2)]
                        v.tensor_tensor(xRest[:, b, :].rearrange("p (g t) -> p g t", g=2),
                                        psum[:, 4 + b, 0:2 * TOKENS].rearrange("p (g t) -> p g t", g=2),
                                        c.unsqueeze(2).broadcast_to([P, 2, TOKENS]),
                                        ALU.add).then_inc(rest_out[b], 1)
                    if r:
                        stats_main(i, r - 1)
                stats_main(i, RING - 1)
                for b in range(2):
                    v.wait_ge(rest_out[b], i + 1)
                    v.bn_stats(stRest[:, bass.ds(12 * i + 6 * b, 6)], xRest[:, b, :]
                               ).then_inc(st_rest_done[b], 1)

            def finish(layer, gamma, beta, sc):
                link(v.tensor_scalar(col(8), col(8), EPS, None, ALU.add))
                v.memset(tmp[:, 15:16], 0.0).then_inc(root_in, 1)
                v.wait_ge(root_out, layer)
                link(v.reciprocal(col(11), col(9)))
                link(v.tensor_tensor(col(12), col(11), col(11), ALU.mult))
                link(v.tensor_tensor(col(12), col(12), col(8), ALU.mult))
                link(v.tensor_scalar(col(12), col(12), -0.5, 1.5, ALU.mult, ALU.add))
                link(v.tensor_tensor(col(11), col(11), col(12), ALU.mult))
                link(v.tensor_tensor(sc[:, 0:1], col(11), par[:, gamma:gamma + 1], ALU.mult))
                link(v.tensor_tensor(col(12), col(10), sc[:, 0:1], ALU.mult))
                link(v.tensor_tensor(sc[:, 1:2], par[:, beta:beta + 1], col(12), ALU.subtract))

            def guarded(alpha, sc):
                link(v.tensor_scalar(col(12), par[:, alpha:alpha + 1], -1.0, 1.0, ALU.mult, ALU.add))
                link(v.tensor_scalar(col(13), col(12), 0.0, TINY, ALU.is_equal, ALU.mult))
                link(v.tensor_tensor(col(12), col(12), col(13), ALU.add))
                link(v.reciprocal(col(13), col(12)))
                link(v.tensor_tensor(sc[:, 2:3], col(13), par[:, alpha:alpha + 1], ALU.mult))

            def signal(s):
                v.memset(tmp[:, 15:16], 0.0).then_inc(s, 1)

            def spread(src_mean, src_var, avg, dst):
                link(v.tensor_tensor(col(7), col(src_mean), psum[:, 6, avg:avg + 1], ALU.subtract))
                link(v.tensor_tensor(col(7), col(7), col(7), ALU.mult))
                link(v.tensor_tensor(col(dst), col(7), col(src_var), ALU.add))

            for r in range(RING):
                v.wait_ge(st_main_done[r], BLOCKS)
            for b in range(2):
                v.wait_ge(st_rest_done[b], BLOCKS)
            link(v.bn_aggr(tmp[:, 0:2], stMain))
            link(v.bn_aggr(tmp[:, 2:4], stRest))
            signal(stat_in)
            v.wait_ge(stat_sum, 1)
            spread(0, 1, 0, 4)
            spread(2, 3, 3, 6)
            signal(stat_in)
            v.wait_ge(stat_sum, 2)
            link(v.tensor_copy(col(10, H1), psum[0:H1, 6, 1:2]))
            link(v.tensor_copy(col(8, H1), psum[0:H1, 6, 2:3]))
            finish(1, Q_G1, Q_BE1, sc1)
            guarded(Q_AL1, sc1)
            link(v.tensor_scalar(w2d[0:H1, 0:H2], par[0:H1, Q_W2:Q_W2 + H2], tmp[0:H1, 12:13], None, ALU.mult))
            link(v.tensor_scalar(w2a[0:H1, 0:H2], par[0:H1, Q_W2:Q_W2 + H2], par[0:H1, Q_AL1:Q_AL1 + 1], None,
                                 ALU.mult))
            signal(dice_ready)

            c0 = 2 * COLS - COLS // 2

            def gate1(i, r):
                v.wait_ge(p1_ready[r], i + 1)
                v.scalar_tensor_tensor(out=h1[0:H1, r, 0:c0], in0=h1[0:H1, r, 0:c0], scalar=sc1[0:H1, 2:3],
                                       in1=x1[0:H1, r, 0:c0], op0=ALU.add, op1=ALU.mult
                                       ).then_inc(h1_ready[r], 1)

            def stats_x2(i, r):
                v.wait_ge(x2_out[r], i + 1)
                for a in range(2):
                    last = v.bn_stats(st2[:, bass.ds(12 * (RING * i + r) + 6 * a, 6)],
                                      x2[:, r, a * 2 * TOKENS:(a + 1) * 2 * TOKENS])
                last.then_inc(st2_done[r], 1)

            for r in range(RING):
                gate1(0, r)
                if r >= 3:
                    stats_x2(0, r - 3)
            with v.Fori(1, BLOCKS) as i:
                for r in range(RING):
                    gate1(i, r)
                    stats_x2(i if r >= 3 else i - 1, (r - 3) % RING)
            for r in (1, 2, 3):
                stats_x2(BLOCKS - 1, r)

            for r in range(RING):
                v.wait_ge(st2_done[r], BLOCKS)
            link(v.bn_aggr(tmp[:, 0:2], st2))
            signal(stat_in)
            v.wait_ge(stat_sum, 3)
            spread(0, 1, 0, 4)
            signal(stat_in)
            v.wait_ge(stat_sum, 4)
            link(v.tensor_copy(col(10, 2 * H2), psum[0:2 * H2, 6, 1:2]))
            link(v.tensor_copy(col(8, 2 * H2), psum[0:2 * H2, 6, 2:3]))
            finish(2, Q_G2, Q_BE2, sc2)
            guarded(Q_AL2, sc2)
            link(v.tensor_scalar(w3z[0:2 * H2, 30:32], par[0:2 * H2, Q_W3A:Q_W3A + 2], tmp[0:2 * H2, 12:13],
                                 None, ALU.mult))
            signal(dice_ready)

            with v.Fori(0, FULLS) as F:
                for t in range(FULL):
                    q = t % RING_C
                    v.wait_ge(p2_ready[q], (FULL // RING_C) * F + (t // RING_C + 1))
                    v.scalar_tensor_tensor(out=p2[0:2 * H2, q, :], in0=p2[0:2 * H2, q, :],
                                           scalar=sc2[0:2 * H2, 2:3],
                                           in1=x2c[0:2 * H2, q, :, :].rearrange("p g n -> p (g n)"),
                                           op0=ALU.add, op1=ALU.mult).then_inc(h2_ready[q], 1)
                v.wait_ge(x3_done[(FULL - 1) % RING_C], (FULL // RING_C) * F + FULL // RING_C)
                v.tensor_scalar(x3[:, bass.ds(2 * TOKENS * F, 2 * TOKENS)], psum[:, 0, 0:2 * TOKENS],
                                par[:, Q_B3:Q_B3 + 1], None, ALU.add).then_inc(x3_out, 1)

            v.wait_ge(x3_out, FULLS)
            for F in range(FULLS):
                link(v.bn_stats(st3[:, 6 * F:6 * F + 6], x3[:, 2 * TOKENS * F:2 * TOKENS * (F + 1)]))
            link(v.bn_aggr(tmp[:, 0:2], st3[:, :]))
            signal(stat_in)
            v.wait_ge(stat_sum, 5)
            link(v.tensor_copy(col(10), psum[:, 6, 0:1]))
            spread(0, 1, 0, 4)
            signal(stat_in)
            v.wait_ge(stat_sum, 6)
            link(v.tensor_copy(col(8), psum[:, 6, 1:2]))
            finish(3, Q_G3, Q_BE3, sc3)
            link(v.tensor_scalar(col(12), par[:, Q_AL3:Q_AL3 + 1], -1.0, 1.0, ALU.mult, ALU.add))
            signal(dice_ready)
            v.wait_ge(p3_ready, 1)
            v.wait_ge(mask_loaded, 16)
            link(v.tensor_scalar(s3, s3, tmp[:, 12:13], par[:, Q_AL3:Q_AL3 + 1], ALU.mult, ALU.add))
            link(v.tensor_tensor(s3, s3, x3, ALU.mult))
            link(v.tensor_scalar(x3, maskI, -1.0, 1.0, ALU.mult, ALU.add))
            v.tensor_tensor(s3, s3, x3, ALU.mult).then_inc(s_ready, 1)

            v.memset(sT[:, :, BATCHES:BATCHES + 32], 0.0).then_inc(sT_out, 1)
            for n in range(2 * FULLS):
                v.wait_ge(sT_done, n + 1)
                for c, m in enumerate(CHUNKS):
                    v.tensor_copy(sT[0:m, c, P * n:P * (n + 1)],
                                  psum[0:m, 2 + n % 2, c * P:(c + 1) * P]).then_inc(sT_out, 1)

            def sums_out(i, s):
                for r in range(RING_D):
                    v.wait_ge(o_done[r], i + 1)
                    if r == 0:
                        v.wait_ge(out_stored[s], 64 * (i - s))
                    v.tensor_copy(oD[:, s, r, :], psum[:, 4 + r, :]).then_inc(o_out[r], 1)

            with v.Fori(0, UNITS // RING_D // 2) as i2:
                for s in range(2):
                    sums_out(2 * i2 + s, s)


SMALL_C = 18


def kernel(**inputs):
    import numpy as np
    import concourse.bacc as bacc
    from concourse.bass_utils import run_bass_kernel_spmd as run

    f32 = np.float32
    a = {k: np.asarray(v) for k, v in inputs.items()}
    w = {k[len("L0_rec_"):]: v for k, v in a.items() if k.startswith("L0_rec_")}
    keys, queries, mask = a["r_keys"], a["r_queries"], a["r_mask"]

    keysT = np.ascontiguousarray(keys.reshape(GROUPS, 2, 4, TOKENS, E).transpose(0, 1, 4, 2, 3)
                                 ).reshape(GROUPS, P, COLS)
    queriesT = np.ascontiguousarray(queries.reshape(GROUPS, 2, 4, E).transpose(1, 3, 0, 2)).reshape(P, 4 * GROUPS)
    order = (8, 16, 2, 2, 2, 2)
    keysU = np.ascontiguousarray(
        keys.reshape(*order, TOKENS, E).transpose(0, 5, 2, 4, 1, 3, 6, 7)
        .reshape(UNITS, 4, 8, TOKENS, E).transpose(0, 3, 1, 2, 4)).reshape(UNITS, TOKENS, 4, BANK)
    maskU = np.ascontiguousarray(mask.reshape(*order, TOKENS).transpose(2, 4, 1, 3, 0, 5, 6)
                                 ).reshape(P, FULLS * 2 * TOKENS)

    par = np.zeros((P, Q_COLS), f32)
    par[:, Q_B1A] = np.tile(w["b1"][:MAIN], 2)
    par[:, Q_B1B] = np.tile(w["b1"][MAIN:], 8)
    for at, name in ((Q_G1, "g1"), (Q_BE1, "be1"), (Q_AL1, "alpha1")):
        par[:H1, at] = w[name]
    for h in range(2):
        par[64 * h:64 * h + H2, Q_B2] = w["b2"]
        par[H2 * h:H2 * h + H2, Q_W3A + h] = w["W3"][:, 0]
    for at, name in ((Q_G2, "g2"), (Q_BE2, "be2"), (Q_AL2, "alpha2")):
        par[:2 * H2, at] = np.tile(w[name], 2)
    for at, name in ((Q_B3, "b3"), (Q_G3, "g3"), (Q_BE3, "be3"), (Q_AL3, "alpha3")):
        par[:, at] = np.tile(w[name], P)
    par[:H1, Q_W2:] = w["W2"]

    con = np.zeros((P, K_COLS), f32)
    p = np.arange(P)
    chA, chB = p % MAIN, MAIN + p % REST
    ch2 = np.where(p % 64 < H2, p % 64, -1 - p)
    con[:, K_ID:K_ID + P] = np.eye(P)
    con[:, K_GA:K_GA + P] = (chA[:, None] == chA) / 2
    con[:, K_GB:K_GB + P] = (chB[:, None] == chB) / 8
    con[:, K_SA:K_SA + H1] = (chA[:, None] == np.arange(H1)) / 2
    con[:, K_SB:K_SB + H1] = (chB[:, None] == np.arange(H1)) / 8
    con[:, K_G2:K_G2 + P] = (ch2[:, None] == ch2) / 2
    con[:, K_S2:K_S2 + 2 * H2] = (ch2[:, None] == np.arange(2 * H2) % H2) / 2
    con[:, K_G3:K_G3 + P] = 1 / P

    nc = bacc.Bacc("TRN2", target_bir_lowering=False, num_devices=1)
    arrays, args = {}, []
    for name, x in (("keysT", keysT), ("keysU", keysU), ("queriesT", queriesT), ("mask", maskU),
                    ("w1", w["W1"]), ("params", par), ("consts", con)):
        arrays[name] = np.ascontiguousarray(x)
        args.append(nc.dram_tensor(name, x.shape, mybir.dt.from_np(x.dtype), kind="ExternalInput").ap())
    args.append(nc.dram_tensor("x1_main", (GROUPS, P, COLS), F32, kind="Internal").ap())
    args.append(nc.dram_tensor("x1_rest", (GROUPS // 2, P, 2 * TOKENS), F32, kind="Internal").ap())
    args.append(nc.dram_tensor("x2_dram", (GROUPS, 2 * H2, COLS), F32, kind="Internal").ap())
    args.append(nc.dram_tensor("out", (UNITS, 4, 8, E), F32, kind="ExternalOutput").ap())
    mask_dice_attention(nc, *args)
    got = run(nc, [arrays], core_ids=[0]).results[0]["out"]
    return np.ascontiguousarray(got.reshape(8, 2, 2, 2, 16, 2, E).transpose(0, 4, 2, 5, 3, 1, 6)
                                ).reshape(BATCHES, 1, E)
```

```python
from contextlib import ExitStack

import concourse.bass as bass
from concourse import mybir

F32 = mybir.dt.float32
I32 = mybir.dt.int32
ALU = mybir.AluOpType
ACT = mybir.ActivationFunctionType

P = 128
BATCHES, TOKENS, E = 2048, 200, 64
H1, H2 = 80, 40
EPS = 1e-8
TINY = 2.0 ** -40
BANK = 512

GROUPS = BATCHES // 8
COLS = 4 * TOKENS
RING = 4
BLOCKS = GROUPS // RING
RING_X = 8
BLOCKS_X = GROUPS // RING_X
MAIN = 64
REST = H1 - MAIN
MCOLS = 2 * H1

TILES_C = GROUPS // 2
FULL = 16
FULLS = TILES_C // FULL
RING_C = 4
RING_Y = 8

UNITS = BATCHES // 32
RING_D = 4
POOL_B = 400
POOL_C = 240
CUT_B = COLS - POOL_B
CUT_C = 2 * COLS - POOL_C
X3_HALF = FULLS * TOKENS
CHUNKS = (96, 104)
CH = max(CHUNKS)

K_ID = 0
K_GA = K_ID + P
K_GB = K_GA + P
K_SA = K_GB + P
K_SB = K_SA + H1
K_G2 = K_SB + H1
K_S2 = K_G2 + P
K_G3 = K_S2 + 2 * H2
K_COLS = K_G3 + P

(Q_B1A, Q_B1B, Q_G1, Q_BE1, Q_AL1, Q_B2, Q_G2, Q_BE2, Q_AL2, Q_W3A, Q_W3B, Q_B3, Q_G3, Q_BE3,
 Q_AL3, Q_W2) = range(16)
Q_COLS = Q_W2 + H2


def mask_dice_attention(nc, keysT, keysU, queriesT, mask, w1, params, consts, x1_main, x1_rest, x2_dram, out):
    with ExitStack() as ctx:
        def sb(name, shape, dt=F32):
            return ctx.enter_context(nc.sbuf_tensor(name, shape, dt))

        def sem(name):
            return ctx.enter_context(nc.semaphore(name))

        def sems(name, n):
            return [sem(f"{name}{r}") for r in range(n)]

        psum = ctx.enter_context(nc.psum_tensor("psum", [P, 8, BANK], F32))

        con = sb("con", [P, K_COLS])
        par = sb("par", [P, Q_COLS])
        w1s = sb("w1s", [P, 4, H1])
        wA = sb("wA", [P, H1])
        wArest = sb("wArest", [P, 2 * REST])
        wB = sb("wB", [P, MCOLS])
        wD = sb("wD", [P, MCOLS])
        tmp = sb("tmp", [P, 16])
        w2d = sb("w2d", [P, 64])
        w2a = sb("w2a", [P, 64])
        w3z = sb("w3z", [P, 62])
        sc1 = sb("sc1", [P, 4])
        sc2 = sb("sc2", [P, 4])
        sc3 = sb("sc3", [P, 4])

        n_x3 = FULLS * 2 * TOKENS
        n_ad = max(RING * (COLS + 4 * MCOLS + COLS) + 2 * 2 * TOKENS + 2 * (GROUPS * 4) + GROUPS,
                   RING_X * 2 * COLS, RING_D * 2 * 4 * BANK)
        n_bc = (RING_Y + RING_C) * 2 * COLS + 3 * n_x3
        arena_ad = sb("arena_ad", [P, n_ad])
        arena_bc = sb("arena_bc", [P, n_bc])

        def cutter(arena):
            at = [0]

            def cut(n):
                at[0] += n
                return arena[:, at[0] - n:at[0]]
            return cut

        cut = cutter(arena_ad)
        keysA = cut(RING * COLS).rearrange("p (r n) -> p r n", r=RING)
        wM = cut(RING * 4 * MCOLS).rearrange("p (r j m) -> p r j m", r=RING, j=4)
        xMain = cut(RING * COLS).rearrange("p (r n) -> p r n", r=RING)
        xRest = cut(2 * 2 * TOKENS).rearrange("p (r n) -> p r n", r=2)
        qT = cut(GROUPS * 4)
        cMain = cut(GROUPS * 4)
        cRest = cut(GROUPS)

        cut = cutter(arena_ad)
        keysD = cut(RING_D * 2 * 4 * BANK).rearrange("p (r c t n) -> p r c t n", r=RING_D, c=2, t=4)

        x1 = cutter(arena_ad)(RING_X * 2 * COLS).rearrange("p (r n) -> p r n", r=RING_X)
        cut = cutter(arena_bc)
        h1 = cut(RING * 2 * COLS).rearrange("p (r n) -> p r n", r=RING)
        x2 = cut(RING_X * COLS).rearrange("p (r n) -> p r n", r=RING_X)
        stMain = cut(6 * 2 * GROUPS)
        stRest = cut(6 * GROUPS // 2)

        cut = cutter(arena_bc)
        x2c = cut(RING_Y * 2 * COLS).rearrange("p (r g n) -> p r g n", r=RING_Y, g=2)
        s3 = cut(n_x3)
        maskI = s3.bitcast(I32)
        x3 = cut(n_x3)
        maskF = cut(n_x3)
        p2 = cut(RING_C * 2 * COLS).rearrange("p (r n) -> p r n", r=RING_C)
        st2 = p2.rearrange("p r n -> p (r n)")[:, 0:12 * GROUPS]

        cut = cutter(arena_bc)
        sT = cut(2 * (BATCHES + 32)).rearrange("p (c n) -> p c n", c=2)
        sU = cut(RING_D * 2 * 64).rearrange("p (r c n) -> p r c n", r=RING_D, c=2)
        oD = arena_bc[:, RING_Y * 2 * COLS + n_x3:][:, 0:2 * RING_D * BANK].rearrange(
            "p (s u n) -> p s u n", s=2, u=RING_D)
        st3 = sb("st3", [P, 6 * FULLS])

        const_loaded = sem("const_loaded")
        keysA_loaded = sems("keysA_loaded", RING)
        x1main_stored = sems("x1main_stored", RING)
        x1rest_stored = sems("x1rest_stored", 2)
        x1_loaded = sems("x1_loaded", RING_X)
        x2_stored = sems("x2_stored", RING_X // 2)
        x2c_loaded = sems("x2c_loaded", RING_Y)
        mask_loaded = sem("mask_loaded")
        keysD_loaded = sems("keysD_loaded", RING_D)
        out_stored = sems("out_stored", 2)
        small = sem("small")
        setup_done = sem("setup_done")
        c_ready = sem("c_ready")
        wM_built = sems("wM_built", RING)
        wM_scaled = sems("wM_scaled", RING)
        x1_done = sems("x1_done", RING)
        main_out = sems("main_out", 2)
        rest_out = sems("rest_out", 2)
        st_main_done = sems("st_main_done", RING)
        st_rest_done = sems("st_rest_done", 2)
        stat_in = sem("stat_in")
        stat_sum = sem("stat_sum")
        root_in = sem("root_in")
        root_out = sem("root_out")
        dice_ready = sem("dice_ready")
        p1_ready = sems("p1_ready", RING)
        h1_ready = sems("h1_ready", RING_X)
        y1_ready = sems("y1_ready", RING_X)
        x2_done = sems("x2_done", RING)
        x2_out = sems("x2_out", RING)
        st2_done = sems("st2_done", RING)
        p2_ready = sems("p2_ready", RING_C)
        h2_ready = sems("h2_ready", RING_Y)
        y2_ready = sems("y2_ready", RING_Y)
        pool_c = sem("pool_c")
        mask_ready = sem("mask_ready")
        xm_ready = sem("xm_ready")
        x3_done = sems("x3_done", RING_C)
        x3_out = sem("x3_out")
        p3_ready = sem("p3_ready")
        s_ready = sem("s_ready")
        sT_done = sem("sT_done")
        sT_out = sems("sT_out", 2)
        sU_ready = sems("sU_ready", RING_D)
        o_done = sems("o_done", RING_D)
        o_out = sems("o_out", RING_D)

        def wait_reuse(eng, s, n):
            if not (isinstance(n, int) and n == 0):
                eng.wait_ge(s, n)

        block = ctx.enter_context(nc.Block())

        @block.sync
        def _(sp):
            sp.dma_start(con[:, :], consts).then_inc(const_loaded, 16)
            sp.dma_start(par[:, :], params).then_inc(const_loaded, 16)
            w1_v = w1.rearrange("(i e) c -> e i c", i=4)
            for h in range(2):
                sp.dma_start(w1s[64 * h:64 * h + 64, :, :], w1_v).then_inc(const_loaded, 16)
            sp.dma_start(qT, queriesT).then_inc(const_loaded, 16)

            def load_keys(i, r):
                sp.dma_start(keysA[:, r, :], keysT[bass.ds(RING * i + r, 1), :, :]
                             .rearrange("a p n -> (a p) n")).then_inc(keysA_loaded[r], 16)

            def store_x1(i, r):
                sp.wait_ge(main_out[r % 2], 2 * i + (r // 2 + 1))
                sp.dma_start(x1_main[bass.ds(RING * i + r, 1), :, :].rearrange("a p n -> (a p) n"),
                             xMain[:, r, :]).then_inc(x1main_stored[r], 16)
                if r % 2:
                    b = r // 2
                    sp.wait_ge(rest_out[b], i + 1)
                    sp.dma_start(x1_rest[bass.ds(2 * i + b, 1), :, :].rearrange("a p n -> (a p) n"),
                                 xRest[:, b, :]).then_inc(x1rest_stored[b], 16)

            for r in range(RING):
                load_keys(0, r)
            with sp.Fori(1, BLOCKS) as i:
                for r in range(RING):
                    sp.wait_ge(x1_done[r], i)
                    load_keys(i, r)
                    store_x1(i - 1, r)
            for r in range(RING):
                store_x1(BLOCKS - 1, r)

            for r in range(RING):
                sp.wait_ge(x1main_stored[r], 16 * BLOCKS)
            for b in range(2):
                sp.wait_ge(x1rest_stored[b], 16 * BLOCKS)

            for r in range(RING):
                sp.wait_ge(st_main_done[r], BLOCKS)
            for b in range(2):
                sp.wait_ge(st_rest_done[b], BLOCKS)

            def load_x1(i, r):
                sp.dma_start(x1[0:MAIN, r, :].rearrange("c (h n) -> c h n", h=2),
                             x1_main[bass.ds(RING_X * i + r, 1), :, :]
                             .rearrange("a (h c) n -> (a c) h n", h=2)).then_inc(x1_loaded[r], 16)
                g = r % 2
                rest = x1_rest[bass.ds(RING_X // 2 * i + r // 2, 1), :, g * TOKENS:(g + 1) * TOKENS]
                for h in range(2):
                    sp.dma_start(x1[MAIN:H1, r, h * COLS:(h + 1) * COLS].rearrange("c (j t) -> c j t", j=4),
                                 rest.rearrange("a (j h c) t -> h (a c) j t", j=4, h=2)[h]
                                 ).then_inc(x1_loaded[r], 16)

            def store_x2(i, r):
                for g in (r - 1, r):
                    sp.wait_ge(x2_out[g % RING], 2 * i + (r // RING + 1))
                for h in range(2):
                    sp.dma_start(x2_dram[bass.ds(RING_X * i + r - 1, 2), h * H2:(h + 1) * H2, :]
                                 .rearrange("g c n -> c g n"),
                                 x2[64 * h:64 * h + H2, r - 1:r + 1, :]).then_inc(x2_stored[r // 2], 16)

            def blocks_b(i, first):
                for r in range(RING_X):
                    sp.wait_ge(x2_done[r % RING], 2 * (i - 1) + (r // RING + 1))
                    load_x1(i, r)
                    if r == 1:
                        if not first:
                            store_x2(i - 2, RING_X - 1)
                    elif r % 2:
                        store_x2(i - 1, r - 2)

            for r in range(RING_X):
                load_x1(0, r)
            blocks_b(1, True)
            with sp.Fori(2, BLOCKS_X) as i:
                blocks_b(i, False)
            store_x2(BLOCKS_X - 2, RING_X - 1)
            for r in range(1, RING_X, 2):
                store_x2(BLOCKS_X - 1, r)

            for b in range(RING_X // 2):
                sp.wait_ge(x2_stored[b], 32 * BLOCKS_X)
            for r in range(RING):
                sp.wait_ge(st2_done[r], BLOCKS)
            sp.dma_start(maskI, mask).then_inc(mask_loaded, 16)

            def load_x2(F, t):
                q = t % RING_Y
                if not (isinstance(F, int) and t < RING_Y):
                    use = (FULL // RING_Y) * F + t // RING_Y
                    sp.wait_ge(h2_ready[q], use)
                    sp.wait_ge(y2_ready[q], use)
                sp.dma_start(x2c[0:2 * H2, q, :, :],
                             x2_dram[bass.ds(2 * (FULL * F + t), 2), :, :].rearrange("g c n -> c g n")
                             ).then_inc(x2c_loaded[q], 16)

            def load_unit(i, r):
                for c, n in enumerate(CHUNKS):
                    sp.dma_start(keysD[0:n, r, c, :, :],
                                 keysU[bass.ds(RING_D * i + r, 1), c * CHUNKS[0]:c * CHUNKS[0] + n, :, :]
                                 .rearrange("a p t n -> (a p) t n")).then_inc(keysD_loaded[r], 16)

            for t in range(RING_Y):
                load_x2(0, t)
            for r in range(RING_D):
                load_unit(0, r)
            for t in range(RING_Y, FULL):
                load_x2(0, t)
            with sp.Fori(1, FULLS) as F:
                for t in range(FULL):
                    load_x2(F, t)

            def store_out(i, s):
                for b in range(8):
                    sp.dma_start(out[bass.ds(RING_D * i, RING_D), :, b, :].rearrange("u t e -> t u e"),
                                 oD[b:b + 97:32, s, :, E * b:E * b + E]).then_inc(out_stored[s], 16)

            def blocks_d(i, s):
                for r in range(RING_D):
                    sp.wait_ge(o_done[r], i)
                    load_unit(i, r)
                for r in range(RING_D):
                    sp.wait_ge(o_out[r], i)
                store_out(i - 1, s)

            n_d = UNITS // RING_D
            with sp.Fori(0, n_d // 2 - 1) as i2:
                blocks_d(2 * i2 + 1, 0)
                blocks_d(2 * i2 + 2, 1)
            blocks_d(n_d - 1, 0)
            for r in range(RING_D):
                sp.wait_ge(o_out[r], n_d)
            store_out(n_d - 1, 1)
            for s in range(2):
                sp.wait_ge(out_stored[s], 16 * 8 * (n_d // 2))

        @block.gpsimd
        def _(pool):
            pool.wait_ge(setup_done, 1)

            def add_wB(i, r):
                pool.wait_ge(wM_scaled[r], i + 1)
                pool.tensor_tensor(wM[:, r, :, :], wM[:, r, :, :],
                                   wB[:, :].unsqueeze(1).broadcast_to([P, 4, MCOLS]),
                                   ALU.add).then_inc(wM_built[r], 1)

            with pool.Fori(0, BLOCKS) as i:
                for r in range(RING):
                    add_wB(i, r)

            def gate1_pool(i, r):
                pool.wait_ge(p1_ready[r % RING], 2 * i + (r // RING + 1))
                y = h1[0:H1, r % RING, :].rearrange("p (h n) -> p h n", h=2)[:, :, CUT_B:]
                pool.tensor_tensor(y, y, x1[0:H1, r, :].rearrange("p (h n) -> p h n", h=2)[:, :, CUT_B:],
                                   ALU.mult).then_inc(y1_ready[r], 1)

            with pool.Fori(0, BLOCKS_X) as i:
                for r in range(RING_X):
                    gate1_pool(i, r)

            beta2 = sc2[0:2 * H2, 2:3].broadcast_to([2 * H2, POOL_C])
            pool.wait_ge(mask_loaded, 16)
            pool.tensor_scalar(maskF, maskI, -1.0, 1.0, ALU.mult, ALU.add).then_inc(mask_ready, 1)

            with pool.Fori(0, FULLS) as F:
                for t in range(FULL):
                    q = t % RING_C
                    pool.wait_ge(p2_ready[q], (FULL // RING_C) * F + (t // RING_C + 1))
                    y = p2[0:2 * H2, q, CUT_C:]
                    pool.tensor_tensor(y, y, beta2, ALU.add).then_inc(pool_c, 1)
                    pool.wait_ge(pool_c, FULL * F + (t + 1))
                    pool.tensor_tensor(y, y, x2c[0:2 * H2, t % RING_Y, 1, CUT_C - COLS:], ALU.mult
                                       ).then_inc(y2_ready[t % RING_Y], 1)
            pool.wait_ge(x3_out, FULLS)
            pool.wait_ge(mask_ready, 1)
            for n in range(2):
                pool.tensor_tensor(maskF[:, n * X3_HALF:(n + 1) * X3_HALF], maskF[:, n * X3_HALF:(n + 1) * X3_HALF],
                                   x3[:, n * X3_HALF:(n + 1) * X3_HALF], ALU.mult).then_inc(xm_ready, 1)

        @block.tensor
        def _(pe):
            pe.wait_ge(setup_done, 1)
            half = GROUPS * 2
            for n in range(2):
                for h in range(2):
                    rows = slice(64 * h, 64 * h + 64)
                    pe.matmul(psum[rows, n, 0:half], wA[rows, 0:MAIN], qT[rows, n * half:(n + 1) * half],
                              start=True, stop=True)
            qj = qT.rearrange("p (g j) -> p j g", j=4)
            for j in range(4):
                last = pe.matmul(psum[32 * j:32 * j + 32, 2, 0:GROUPS], wArest[:, :], qj[:, j, :],
                                 start=True, stop=True)
            last.then_inc(c_ready, 1)
            pe.wait_ge(small, SMALL_C)

            def x1_group(i, r):
                s, b = r % 2, r // 2
                pe.wait_ge(keysA_loaded[r], 16 * i + 16)
                wait_reuse(pe, main_out[s], 2 * i + r // 2)
                if s == 0:
                    wait_reuse(pe, rest_out[b], i)
                pe.wait_ge(wM_built[r], i + 1)
                for j in range(4):
                    c = (j % 2) * TOKENS
                    pe.matmul(psum[:, 2 * s + j // 2, c:c + TOKENS], wM[:, r, j, 0:2 * MAIN],
                              keysA[:, r, j * TOKENS:(j + 1) * TOKENS], start=True, stop=True)
                for j in range(4):
                    last = pe.matmul(psum[32 * j:32 * j + 32, 4 + b, s * TOKENS:(s + 1) * TOKENS],
                                     wM[:, r, j, 2 * MAIN:MCOLS], keysA[:, r, j * TOKENS:(j + 1) * TOKENS],
                                     start=True, stop=True)
                last.then_inc(x1_done[r], 1)

            for r in range(RING):
                x1_group(0, r)
            with pe.Fori(1, BLOCKS) as i:
                for r in range(RING):
                    x1_group(i, r)

            def averages(step, outs):
                pe.wait_ge(stat_in, step)
                for col, terms in outs:
                    for n, (k, m, v) in enumerate(terms):
                        last = pe.matmul(psum[0:m, 6, col:col + 1], con[:, k:k + m], tmp[:, v:v + 1],
                                         start=(n == 0), stop=(n == len(terms) - 1))
                last.then_inc(stat_sum, 1)

            def warm_up():
                for _ in range(4):
                    pe.matmul(psum[:, 7, :], con[:, 0:P], con[:, 0:BANK], start=True, stop=True)

            averages(1, [(0, [(K_GA, P, 0)]), (3, [(K_GB, P, 2)])])
            averages(2, [(1, [(K_SA, H1, 0), (K_SB, H1, 2)]), (2, [(K_SA, H1, 4), (K_SB, H1, 6)])])

            warm_up()
            pe.wait_ge(dice_ready, 1)

            def x2_group(i, r):
                q = r % RING
                wait_reuse(pe, x2_out[q], 2 * i + r // RING)
                pe.wait_ge(h1_ready[r], i + 1)
                x = (h1[0:H1, q, :], x1[0:H1, r, :])
                for a in range(2):
                    if a == 1:
                        pe.wait_ge(y1_ready[r], i + 1)
                    for h in range(2):
                        c = h * COLS + a * (COLS // 2)
                        pe.matmul(psum[64 * h:64 * h + 64, 2 * q + a, 0:COLS // 2], w2d[0:H1, :],
                                  x[0][:, c:c + COLS // 2], start=True, stop=(a == 0))
                for h in range(2):
                    last = pe.matmul(psum[64 * h:64 * h + 64, 2 * q + 1, COLS // 2 - POOL_B:COLS // 2],
                                     w2a[0:H1, :], x[1][:, h * COLS + CUT_B:(h + 1) * COLS],
                                     start=False, stop=True)
                last.then_inc(x2_done[q], 1)

            for r in range(RING_X):
                x2_group(0, r)
            with pe.Fori(1, BLOCKS_X) as i:
                for r in range(RING_X):
                    x2_group(i, r)

            averages(3, [(0, [(K_G2, P, 0)])])
            averages(4, [(1, [(K_S2, 2 * H2, 0)]), (2, [(K_S2, 2 * H2, 4)])])

            warm_up()
            pe.wait_ge(dice_ready, 2)

            def x3_full(F):
                wait_reuse(pe, x3_out, F)
                for t in range(FULL):
                    q = t % RING_C
                    use = (FULL // RING_Y) * F + (t // RING_Y + 1)
                    pe.wait_ge(h2_ready[t % RING_Y], use)
                    for g in range(2):
                        for a in range(2):
                            ct = 2 * g + a
                            c = g * COLS + a * 2 * TOKENS
                            if ct == 3:
                                pe.wait_ge(y2_ready[t % RING_Y], use)
                            last = pe.matmul(psum[32 * ct:32 * ct + 32, 0, 0:2 * TOKENS],
                                             w3z[0:2 * H2, 30 - 2 * t:62 - 2 * t],
                                             p2[0:2 * H2, q, c:c + 2 * TOKENS],
                                             start=(t == 0), stop=(t == FULL - 1))
                    last.then_inc(x3_done[q], 1)

            x3_full(0)
            with pe.Fori(1, FULLS) as F:
                x3_full(F)

            averages(5, [(0, [(K_G3, P, 0)])])
            averages(6, [(1, [(K_G3, P, 4)])])

            for n in range(FULLS):
                pe.wait_ge(s_ready, n + 1)
                if n >= 2:
                    pe.wait_ge(sT_out[0], n)
                    pe.wait_ge(sT_out[1], n - 1)
                for par_ in range(2):
                    c0 = (2 * n + par_) * TOKENS
                    for c, m in enumerate(CHUNKS):
                        last = pe.transpose(psum[0:m, c + 2 * (n % 2), par_ * P:(par_ + 1) * P],
                                            s3[:, c0:c0 + m], con[:, K_ID:K_ID + P])
                        c0 += m
                last.then_inc(sT_done, 1)

            def unit_sums(i, r):
                pe.wait_ge(keysD_loaded[r], 32 * i + 32)
                wait_reuse(pe, o_out[r], i)
                pe.wait_ge(sU_ready[r], i + 1)
                for c, n in enumerate(CHUNKS):
                    for t in range(4):
                        last = pe.matmul(psum[32 * t:32 * t + 32, 4 + r, :], sU[0:n, r, c, 8 * t:8 * t + 32],
                                         keysD[0:n, r, c, t, :], start=(c == 0), stop=(c == 1))
                last.then_inc(o_done[r], 1)

            for r in range(RING_D):
                unit_sums(0, r)
            with pe.Fori(1, UNITS // RING_D) as i:
                for r in range(RING_D):
                    unit_sums(i, r)

        @block.scalar
        def _(act):
            def root(n):
                act.wait_ge(root_in, n)
                act.activation(tmp[:, 9:10], tmp[:, 8:9], ACT.Sqrt).then_inc(root_out, 1)

            def scale_wD(i, r):
                wait_reuse(act, x1_done[r], i)
                act.wait_ge(setup_done, 1)
                for j in range(4):
                    last = act.activation(wM[:, r, j, :], wD[:, :], ACT.Identity, bias=0.0,
                                          scale=qT[:, bass.ds(4 * RING * i + 4 * r + j, 1)])
                last.then_inc(wM_scaled[r], 1)

            for r in range(RING):
                scale_wD(0, r)
            with act.Fori(1, BLOCKS) as i:
                for r in range(RING):
                    scale_wD(i, r)

            root(1)

            act.wait_ge(dice_ready, 1)

            def sigmoid1(i, r):
                q = r % RING
                act.wait_ge(x1_loaded[r], 48 * i + 48)
                wait_reuse(act, x2_done[q], 2 * i + r // RING)
                act.activation(h1[0:H1, q, :], x1[0:H1, r, :], ACT.Sigmoid, bias=sc1[0:H1, 1:2],
                               scale=sc1[0:H1, 0:1]).then_inc(p1_ready[q], 1)

            def x2_from_psum(i, r):
                q, use = r % RING, 2 * i + r // RING
                act.wait_ge(x2_done[q], use + 1)
                wait_reuse(act, x2_stored[r // 2], 32 * i)
                if not (isinstance(i, int) and i == 0):
                    act.wait_ge(st2_done[q], 2 * (i - 1) + (r // RING + 1))
                act.activation(x2[:, r, :].rearrange("p (a n) -> p a n", a=2),
                               psum[:, 2 * q:2 * q + 2, 0:COLS // 2], ACT.Identity,
                               bias=par[:, Q_B2:Q_B2 + 1]).then_inc(x2_out[q], 1)

            for r in range(RING_X):
                sigmoid1(0, r)
                if r >= 2:
                    x2_from_psum(0, r - 2)
            with act.Fori(1, BLOCKS_X) as i:
                for r in range(RING_X):
                    sigmoid1(i, r)
                    x2_from_psum(i if r >= 2 else i - 1, (r - 2) % RING_X)
            for r in (RING_X - 2, RING_X - 1):
                x2_from_psum(BLOCKS_X - 1, r)

            root(2)

            act.wait_ge(dice_ready, 2)

            def sigmoid2(F):
                for t in range(FULL):
                    q = t % RING_C
                    act.wait_ge(x2c_loaded[t % RING_Y], 16 * ((FULL // RING_Y) * F + (t // RING_Y + 1)))
                    wait_reuse(act, x3_done[q], (FULL // RING_C) * F + t // RING_C)
                    act.activation(p2[0:2 * H2, q, :],
                                   x2c[0:2 * H2, t % RING_Y, :, :].rearrange("p g n -> p (g n)"),
                                   ACT.Sigmoid, bias=sc2[0:2 * H2, 1:2], scale=sc2[0:2 * H2, 0:1]
                                   ).then_inc(p2_ready[q], 1)

            sigmoid2(0)
            with act.Fori(1, FULLS) as F:
                sigmoid2(F)

            root(3)
            act.wait_ge(dice_ready, 3)
            act.wait_ge(mask_ready, 1)
            for n in range(4):
                part = slice(n * X3_HALF // 2, (n + 1) * X3_HALF // 2)
                act.activation(s3[:, part], x3[:, part], ACT.Sigmoid, bias=sc3[:, 1:2], scale=sc3[:, 0:1]
                               ).then_inc(p3_ready, 1)

            m = CHUNKS[1]
            for n in range(FULLS):
                act.wait_ge(sT_done, n + 1)
                act.copy(sT[0:m, 1, 2 * P * n:2 * P * (n + 1)], psum[0:m, 1 + 2 * (n % 2), 0:2 * P]
                         ).then_inc(sT_out[1], 1)

            act.wait_ge(sT_out[0], FULLS + 1)
            act.wait_ge(sT_out[1], FULLS)

            def unit_scores(i, r):
                wait_reuse(act, o_done[r], i)
                act.wait_ge(dice_ready, 3)
                for c, n in enumerate(CHUNKS):
                    last = act.copy(sU[0:n, r, c, 0:56], sT[0:n, c, bass.ds(32 * (RING_D * i + r), 56)])
                last.then_inc(sU_ready[r], 1)

            for r in range(RING_D):
                unit_scores(0, r)
            with act.Fori(1, UNITS // RING_D) as i:
                for r in range(RING_D):
                    unit_scores(i, r)

        @block.vector
        def _(v):
            steps = [0]

            def link(ins):
                steps[0] += 1
                ins.then_inc(small, 1)
                v.wait_ge(small, steps[0])

            def col(k, rows=P):
                return tmp[0:rows, k:k + 1]

            v.wait_ge(const_loaded, 80)
            for t in (wB, wD, wArest, w2d, w2a, w3z, tmp):
                link(v.memset(t[:, :], 0.0))
            link(v.tensor_tensor(wA[:, :], w1s[:, 0, :], w1s[:, 2, :], ALU.add))
            for h in range(2):
                rows, main, at = slice(64 * h, 64 * h + 64), MAIN * h, REST * h
                link(v.tensor_copy(wArest[rows, at:at + REST], wA[rows, MAIN:H1]))
                for a, b, n in ((main, 0, MAIN), (2 * MAIN + at, MAIN, REST)):
                    link(v.tensor_tensor(wB[rows, a:a + n], w1s[rows, 1, b:b + n], w1s[rows, 2, b:b + n],
                                         ALU.subtract))
                    link(v.tensor_copy(wD[rows, a:a + n], w1s[rows, 3, b:b + n]))
            v.memset(tmp[:, 15:16], 0.0).then_inc(setup_done, 1)

            v.wait_ge(c_ready, 1)
            link(v.tensor_scalar(cMain.rearrange("p (a n) -> p a n", a=2), psum[:, 0:2, 0:2 * GROUPS],
                                 par[:, Q_B1A:Q_B1A + 1], None, ALU.add))
            link(v.tensor_scalar(cRest, psum[:, 2, 0:GROUPS], par[:, Q_B1B:Q_B1B + 1], None, ALU.add))
            assert steps[0] == SMALL_C

            def stats_main(i, r):
                v.wait_ge(main_out[r % 2], 2 * i + (r // 2 + 1))
                for a in range(2):
                    last = v.bn_stats(stMain[:, bass.ds(12 * (RING * i + r) + 6 * a, 6)],
                                      xMain[:, r, a * 2 * TOKENS:(a + 1) * 2 * TOKENS])
                last.then_inc(st_main_done[r], 1)

            def block_a(i):
                for r in range(RING):
                    s, b = r % 2, r // 2
                    wait_reuse(v, x1main_stored[r], 16 * i)
                    wait_reuse(v, st_main_done[r], i)
                    v.wait_ge(x1_done[r], i + 1)
                    c = cMain[:, bass.ds(4 * (RING * i + r), 4)].rearrange("p (a j) -> p a j", a=2)
                    v.tensor_tensor(xMain[:, r, :].rearrange("p (a j t) -> p a j t", a=2, j=2),
                                    psum[:, 2 * s:2 * s + 2, 0:2 * TOKENS].rearrange("p a (j t) -> p a j t", j=2),
                                    c.unsqueeze(3).broadcast_to([P, 2, 2, TOKENS]),
                                    ALU.add).then_inc(main_out[s], 1)
                    if s == 1:
                        wait_reuse(v, x1rest_stored[b], 16 * i)
                        wait_reuse(v, st_rest_done[b], i)
                        c = cRest[:, bass.ds(RING * i + 2 * b, 2)]
                        v.tensor_tensor(xRest[:, b, :].rearrange("p (g t) -> p g t", g=2),
                                        psum[:, 4 + b, 0:2 * TOKENS].rearrange("p (g t) -> p g t", g=2),
                                        c.unsqueeze(2).broadcast_to([P, 2, TOKENS]),
                                        ALU.add).then_inc(rest_out[b], 1)
                    if r:
                        stats_main(i, r - 1)
                stats_main(i, RING - 1)
                for b in range(2):
                    v.wait_ge(rest_out[b], i + 1)
                    v.bn_stats(stRest[:, bass.ds(12 * i + 6 * b, 6)], xRest[:, b, :]
                               ).then_inc(st_rest_done[b], 1)

            block_a(0)
            with v.Fori(1, BLOCKS) as i:
                block_a(i)

            def finish(layer, gamma, beta, sc):
                link(v.tensor_scalar(col(8), col(8), EPS, None, ALU.add))
                v.memset(tmp[:, 15:16], 0.0).then_inc(root_in, 1)
                v.wait_ge(root_out, layer)
                link(v.reciprocal(col(11), col(9)))
                link(v.tensor_tensor(col(12), col(11), col(11), ALU.mult))
                link(v.tensor_tensor(col(12), col(12), col(8), ALU.mult))
                link(v.tensor_scalar(col(12), col(12), -0.5, 1.5, ALU.mult, ALU.add))
                link(v.tensor_tensor(col(11), col(11), col(12), ALU.mult))
                link(v.tensor_tensor(sc[:, 0:1], col(11), par[:, gamma:gamma + 1], ALU.mult))
                link(v.tensor_tensor(col(12), col(10), sc[:, 0:1], ALU.mult))
                link(v.tensor_tensor(sc[:, 1:2], par[:, beta:beta + 1], col(12), ALU.subtract))

            def guarded(alpha, sc):
                link(v.tensor_scalar(col(12), par[:, alpha:alpha + 1], -1.0, 1.0, ALU.mult, ALU.add))
                link(v.tensor_scalar(col(13), col(12), 0.0, TINY, ALU.is_equal, ALU.mult))
                link(v.tensor_tensor(col(12), col(12), col(13), ALU.add))
                link(v.reciprocal(col(13), col(12)))
                link(v.tensor_tensor(sc[:, 2:3], col(13), par[:, alpha:alpha + 1], ALU.mult))

            def signal(s):
                v.memset(tmp[:, 15:16], 0.0).then_inc(s, 1)

            def spread(src_mean, src_var, avg, dst):
                link(v.tensor_tensor(col(7), col(src_mean), psum[:, 6, avg:avg + 1], ALU.subtract))
                link(v.tensor_tensor(col(7), col(7), col(7), ALU.mult))
                link(v.tensor_tensor(col(dst), col(7), col(src_var), ALU.add))

            for r in range(RING):
                v.wait_ge(st_main_done[r], BLOCKS)
            for b in range(2):
                v.wait_ge(st_rest_done[b], BLOCKS)
            link(v.bn_aggr(tmp[:, 0:2], stMain))
            link(v.bn_aggr(tmp[:, 2:4], stRest))
            signal(stat_in)
            v.wait_ge(stat_sum, 1)
            spread(0, 1, 0, 4)
            spread(2, 3, 3, 6)
            signal(stat_in)
            v.wait_ge(stat_sum, 2)
            link(v.tensor_copy(col(10, H1), psum[0:H1, 6, 1:2]))
            link(v.tensor_copy(col(8, H1), psum[0:H1, 6, 2:3]))
            finish(1, Q_G1, Q_BE1, sc1)
            guarded(Q_AL1, sc1)
            link(v.tensor_scalar(w2d[0:H1, 0:H2], par[0:H1, Q_W2:Q_W2 + H2], tmp[0:H1, 12:13], None, ALU.mult))
            link(v.tensor_scalar(w2a[0:H1, 0:H2], par[0:H1, Q_W2:Q_W2 + H2], par[0:H1, Q_AL1:Q_AL1 + 1], None,
                                 ALU.mult))
            signal(dice_ready)


            def gate1(i, r):
                q = r % RING
                v.wait_ge(p1_ready[q], 2 * i + (r // RING + 1))
                p = h1[0:H1, q, :].rearrange("p (h n) -> p h n", h=2)[:, :, 0:CUT_B]
                x = x1[0:H1, r, :].rearrange("p (h n) -> p h n", h=2)[:, :, 0:CUT_B]
                v.scalar_tensor_tensor(out=p, in0=p, scalar=sc1[0:H1, 2:3], in1=x, op0=ALU.add, op1=ALU.mult
                                       ).then_inc(h1_ready[r], 1)

            def stats_x2(i, r):
                q = r % RING
                v.wait_ge(x2_out[q], 2 * i + (r // RING + 1))
                for a in range(2):
                    last = v.bn_stats(st2[:, bass.ds(12 * (RING_X * i + r) + 6 * a, 6)],
                                      x2[:, r, a * 2 * TOKENS:(a + 1) * 2 * TOKENS])
                last.then_inc(st2_done[q], 1)

            for r in range(RING_X):
                gate1(0, r)
                if r >= 3:
                    stats_x2(0, r - 3)
            with v.Fori(1, BLOCKS_X) as i:
                for r in range(RING_X):
                    gate1(i, r)
                    stats_x2(i if r >= 3 else i - 1, (r - 3) % RING_X)
            for r in (RING_X - 3, RING_X - 2, RING_X - 1):
                stats_x2(BLOCKS_X - 1, r)

            for r in range(RING):
                v.wait_ge(st2_done[r], BLOCKS)
            link(v.bn_aggr(tmp[:, 0:2], st2))
            signal(stat_in)
            v.wait_ge(stat_sum, 3)
            spread(0, 1, 0, 4)
            signal(stat_in)
            v.wait_ge(stat_sum, 4)
            link(v.tensor_copy(col(10, 2 * H2), psum[0:2 * H2, 6, 1:2]))
            link(v.tensor_copy(col(8, 2 * H2), psum[0:2 * H2, 6, 2:3]))
            finish(2, Q_G2, Q_BE2, sc2)
            guarded(Q_AL2, sc2)
            link(v.tensor_scalar(w3z[0:2 * H2, 30:32], par[0:2 * H2, Q_W3A:Q_W3A + 2], tmp[0:2 * H2, 12:13],
                                 None, ALU.mult))
            signal(dice_ready)

            with v.Fori(0, FULLS) as F:
                for t in range(FULL):
                    q = t % RING_C
                    v.wait_ge(p2_ready[q], (FULL // RING_C) * F + (t // RING_C + 1))
                    v.scalar_tensor_tensor(out=p2[0:2 * H2, q, 0:CUT_C], in0=p2[0:2 * H2, q, 0:CUT_C],
                                           scalar=sc2[0:2 * H2, 2:3],
                                           in1=x2c[0:2 * H2, t % RING_Y, :, :].rearrange("p g n -> p (g n)")[:, 0:CUT_C],
                                           op0=ALU.add, op1=ALU.mult).then_inc(h2_ready[t % RING_Y], 1)
                v.wait_ge(x3_done[(FULL - 1) % RING_C], (FULL // RING_C) * F + FULL // RING_C)
                v.tensor_scalar(x3[:, bass.ds(2 * TOKENS * F, 2 * TOKENS)], psum[:, 0, 0:2 * TOKENS],
                                par[:, Q_B3:Q_B3 + 1], None, ALU.add).then_inc(x3_out, 1)

            v.wait_ge(x3_out, FULLS)
            for F in range(FULLS):
                link(v.bn_stats(st3[:, 6 * F:6 * F + 6], x3[:, 2 * TOKENS * F:2 * TOKENS * (F + 1)]))
            link(v.bn_aggr(tmp[:, 0:2], st3[:, :]))
            signal(stat_in)
            v.wait_ge(stat_sum, 5)
            link(v.tensor_copy(col(10), psum[:, 6, 0:1]))
            spread(0, 1, 0, 4)
            signal(stat_in)
            v.wait_ge(stat_sum, 6)
            link(v.tensor_copy(col(8), psum[:, 6, 1:2]))
            finish(3, Q_G3, Q_BE3, sc3)
            guarded(Q_AL3, sc3)
            signal(dice_ready)
            quarter = X3_HALF // 2
            for n in range(4):
                part = slice(n * quarter, (n + 1) * quarter)
                v.wait_ge(p3_ready, n + 1)
                v.wait_ge(xm_ready, n // 2 + 1)
                v.scalar_tensor_tensor(out=s3[:, part], in0=s3[:, part], scalar=sc3[:, 2:3], in1=maskF[:, part],
                                       op0=ALU.add, op1=ALU.mult).then_inc(s_ready, 2)

            m = CHUNKS[0]
            v.memset(sT[:, :, BATCHES:BATCHES + 32], 0.0).then_inc(sT_out[0], 1)
            for n in range(FULLS):
                v.wait_ge(sT_done, n + 1)
                v.tensor_copy(sT[0:m, 0, 2 * P * n:2 * P * (n + 1)], psum[0:m, 2 * (n % 2), 0:2 * P]
                              ).then_inc(sT_out[0], 1)

            def sums_out(i2, s):
                for r in range(RING_D):
                    if r == 0:
                        wait_reuse(v, out_stored[s], 16 * 8 * i2)
                    v.wait_ge(o_done[r], 2 * i2 + (s + 1))
                    v.tensor_scalar(oD[:, s, r, :], psum[:, 4 + r, :], tmp[:, 12:13], None, ALU.mult
                                    ).then_inc(o_out[r], 1)

            for s in range(2):
                sums_out(0, s)
            with v.Fori(1, UNITS // RING_D // 2) as i2:
                for s in range(2):
                    sums_out(i2, s)


SMALL_C = 20


def kernel(**inputs):
    import numpy as np
    import concourse.bacc as bacc
    from concourse.bass_utils import run_bass_kernel_spmd as run

    f32 = np.float32
    a = {k: np.asarray(v) for k, v in inputs.items()}
    w = {k[len("L0_rec_"):]: v for k, v in a.items() if k.startswith("L0_rec_")}
    keys, queries, mask = a["r_keys"], a["r_queries"], a["r_mask"]

    keysT = np.ascontiguousarray(keys.reshape(GROUPS, 2, 4, TOKENS, E).transpose(0, 1, 4, 2, 3)
                                 ).reshape(GROUPS, P, COLS)
    queriesT = np.ascontiguousarray(queries.reshape(GROUPS, 2, 4, E).transpose(1, 3, 0, 2)).reshape(P, 4 * GROUPS)
    order = (8, 16, 2, 2, 2, 2)
    keysU = np.ascontiguousarray(
        keys.reshape(*order, TOKENS, E).transpose(0, 5, 2, 4, 1, 3, 6, 7)
        .reshape(UNITS, 4, 8, TOKENS, E).transpose(0, 3, 1, 2, 4)).reshape(UNITS, TOKENS, 4, BANK)
    maskU = np.ascontiguousarray(mask.reshape(*order, TOKENS).transpose(2, 4, 1, 3, 0, 5, 6)
                                 ).reshape(P, FULLS * 2 * TOKENS)

    par = np.zeros((P, Q_COLS), f32)
    par[:, Q_B1A] = np.tile(w["b1"][:MAIN], 2)
    par[:, Q_B1B] = np.tile(w["b1"][MAIN:], 8)
    for at, name in ((Q_G1, "g1"), (Q_BE1, "be1"), (Q_AL1, "alpha1")):
        par[:H1, at] = w[name]
    for h in range(2):
        par[64 * h:64 * h + H2, Q_B2] = w["b2"]
        par[H2 * h:H2 * h + H2, Q_W3A + h] = w["W3"][:, 0]
    for at, name in ((Q_G2, "g2"), (Q_BE2, "be2"), (Q_AL2, "alpha2")):
        par[:2 * H2, at] = np.tile(w[name], 2)
    for at, name in ((Q_B3, "b3"), (Q_G3, "g3"), (Q_BE3, "be3"), (Q_AL3, "alpha3")):
        par[:, at] = np.tile(w[name], P)
    par[:H1, Q_W2:] = w["W2"]

    con = np.zeros((P, K_COLS), f32)
    p = np.arange(P)
    chA, chB = p % MAIN, MAIN + p % REST
    ch2 = np.where(p % 64 < H2, p % 64, -1 - p)
    con[:, K_ID:K_ID + P] = np.eye(P)
    con[:, K_GA:K_GA + P] = (chA[:, None] == chA) / 2
    con[:, K_GB:K_GB + P] = (chB[:, None] == chB) / 8
    con[:, K_SA:K_SA + H1] = (chA[:, None] == np.arange(H1)) / 2
    con[:, K_SB:K_SB + H1] = (chB[:, None] == np.arange(H1)) / 8
    con[:, K_G2:K_G2 + P] = (ch2[:, None] == ch2) / 2
    con[:, K_S2:K_S2 + 2 * H2] = (ch2[:, None] == np.arange(2 * H2) % H2) / 2
    con[:, K_G3:K_G3 + P] = 1 / P

    nc = bacc.Bacc("TRN2", target_bir_lowering=False, num_devices=1)
    arrays, args = {}, []
    for name, x in (("keysT", keysT), ("keysU", keysU), ("queriesT", queriesT), ("mask", maskU),
                    ("w1", w["W1"]), ("params", par), ("consts", con)):
        arrays[name] = np.ascontiguousarray(x)
        args.append(nc.dram_tensor(name, x.shape, mybir.dt.from_np(x.dtype), kind="ExternalInput").ap())
    args.append(nc.dram_tensor("x1_main", (GROUPS, P, COLS), F32, kind="Internal").ap())
    args.append(nc.dram_tensor("x1_rest", (GROUPS // 2, P, 2 * TOKENS), F32, kind="Internal").ap())
    args.append(nc.dram_tensor("x2_dram", (GROUPS, 2 * H2, COLS), F32, kind="Internal").ap())
    args.append(nc.dram_tensor("out", (UNITS, 4, 8, E), F32, kind="ExternalOutput").ap())
    mask_dice_attention(nc, *args)
    got = run(nc, [arrays], core_ids=[0]).results[0]["out"]
    return np.ascontiguousarray(got.reshape(8, 2, 2, 2, 16, 2, E).transpose(0, 4, 2, 5, 3, 1, 6)
                                ).reshape(BATCHES, 1, E)
```

```python
from contextlib import ExitStack

import concourse.bass as bass
from concourse import mybir

F32 = mybir.dt.float32
I32 = mybir.dt.int32
ALU = mybir.AluOpType
ACT = mybir.ActivationFunctionType

P = 128
BATCHES, TOKENS, E = 2048, 200, 64
H1, H2 = 80, 40
EPS = 1e-8
TINY = 2.0 ** -40
BANK = 512

GROUPS = BATCHES // 8
COLS = 4 * TOKENS
RING = 4
BLOCKS = GROUPS // RING
RING_X = 8
BLOCKS_X = GROUPS // RING_X
BY_V = (3, 7)
POOL_B = 400
CUT_B = COLS - POOL_B
PAIRS = RING_X // 2
MAIN = 64
REST = H1 - MAIN
MCOLS = 2 * H1

TILES_C = GROUPS // 2
FULL = 16
FULLS = TILES_C // FULL
RING_C = 4
RING_Y = 8

UNITS = BATCHES // 32
RING_D = 4
RING_K = 8
BLOCKS_D = UNITS // RING_K
UNIT = 2 * 4 * BANK
POOL_C = 280
CUT_C = 2 * COLS - POOL_C
CHUNKS = (96, 104)

T_A, T_SPREAD, T_VAR, T_ROOT, T_INV, T_NONE = range(4, 16, 2)

K_ID = 0
K_GA = K_ID + P
K_GB = K_GA + P
K_SA = K_GB + P
K_SB = K_SA + H1
K_G2 = K_SB + H1
K_S2 = K_G2 + P
K_G3 = K_S2 + 2 * H2
K_COLS = K_G3 + P

Q_G, Q_BE, Q_AL = 0, 3, 6
Q_B1A, Q_B1B, Q_B2, Q_B3, Q_W3A, Q_W3B = range(9, 15)
Q_W2 = 15
Q_COLS = Q_W2 + H2


def mask_dice_attention(nc, keysT, keysU, queriesT, mask, w1, params, consts, x1_main, x1_rest, x2_dram, out):
    with ExitStack() as ctx:
        def sb(name, shape, dt=F32):
            return ctx.enter_context(nc.sbuf_tensor(name, shape, dt))

        def sem(name):
            return ctx.enter_context(nc.semaphore(name))

        def sems(name, n):
            return [sem(f"{name}{r}") for r in range(n)]

        psum = ctx.enter_context(nc.psum_tensor("psum", [P, 8, BANK], F32))

        con = sb("con", [P, K_COLS])
        par = sb("par", [P, Q_COLS])
        w1s = sb("w1s", [P, 4, H1])
        wA = sb("wA", [P, H1])
        wArest = sb("wArest", [P, 2 * REST])
        wB = sb("wB", [P, MCOLS])
        wD = sb("wD", [P, MCOLS])
        tmp = sb("tmp", [P, 16])
        w2d = sb("w2d", [P, 64])
        w2a = sb("w2a", [P, 64])
        w3z = sb("w3z", [P, 62])
        scale = sb("scale", [P, 3])
        bias = sb("bias", [P, 3])
        beta = sb("beta", [P, 3])
        dd = sb("dd", [P, 3])

        n_x3 = FULLS * 2 * TOKENS
        n_ad = max(RING * (COLS + 4 * MCOLS + COLS) + 2 * 2 * TOKENS + 2 * (GROUPS * 4) + GROUPS,
                   RING_X * 2 * COLS, 4 * UNIT)
        n_bc = RING_Y * 2 * COLS + 3 * n_x3 + 2 * UNIT
        arena_ad = sb("arena_ad", [P, n_ad])
        arena_bc = sb("arena_bc", [P, n_bc])

        def cutter(arena):
            at = [0]

            def cut(n):
                at[0] += n
                return arena[:, at[0] - n:at[0]]
            return cut

        cut = cutter(arena_ad)
        keysA = cut(RING * COLS).rearrange("p (r n) -> p r n", r=RING)
        wM = cut(RING * 4 * MCOLS).rearrange("p (r j m) -> p r j m", r=RING, j=4)
        xMain = cut(RING * COLS).rearrange("p (r n) -> p r n", r=RING)
        xRest = cut(2 * 2 * TOKENS).rearrange("p (r n) -> p r n", r=2)
        qT = cut(GROUPS * 4)
        cMain = cut(GROUPS * 4)
        cRest = cut(GROUPS)

        cut = cutter(arena_bc)
        h1 = cut(RING_X * 2 * COLS).rearrange("p (r n) -> p r n", r=RING_X)
        x2 = cut(RING_X * COLS).rearrange("p (r n) -> p r n", r=RING_X)
        x1 = cutter(arena_ad)(RING_X * 2 * COLS).rearrange("p (r n) -> p r n", r=RING_X)

        cut = cutter(arena_bc)
        x2c = cut(RING_Y * 2 * COLS).rearrange("p (r g n) -> p r g n", r=RING_Y, g=2)
        s3 = cut(n_x3)
        maskI = s3.bitcast(I32)
        x3 = cut(n_x3)
        maskF = cut(n_x3)
        p2 = cut(RING_C * 2 * COLS).rearrange("p (r n) -> p r n", r=RING_C)

        cut = cutter(arena_bc[:, RING_Y * 2 * COLS + 3 * n_x3:])
        st2 = cut(12 * GROUPS)
        stMain = cut(6 * 2 * GROUPS)
        stRest = cut(6 * GROUPS // 2)

        cut = cutter(arena_bc)
        sT = cut(2 * (BATCHES + 32)).rearrange("p (c n) -> p c n", c=2)
        keysD = [arena_ad[:, n * UNIT:(n + 1) * UNIT] for n in range(4)] + [cut(UNIT), cut(UNIT)]
        at = RING_Y * 2 * COLS + 3 * n_x3
        keysD += [arena_bc[:, at + n * UNIT:at + (n + 1) * UNIT] for n in range(2)]
        keysD = [k.rearrange("p (c t n) -> p c t n", c=2, t=4) for k in keysD]
        oD = arena_bc[:, RING_Y * 2 * COLS + n_x3:][:, 0:2 * RING_D * BANK].rearrange(
            "p (s u n) -> p s u n", s=2, u=RING_D)
        sU = sb("sU", [P, RING_D, 2, 64])
        st3 = sb("st3", [P, 6 * FULLS])

        w1_loaded = sem("w1_loaded")
        con_loaded = sem("con_loaded")
        keysA_loaded = sems("keysA_loaded", RING)
        x1main_stored = sems("x1main_stored", RING)
        x1rest_stored = sems("x1rest_stored", 2)
        x1_loaded = sems("x1_loaded", RING_X)
        x2_stored = sems("x2_stored", PAIRS)
        x2c_loaded = sems("x2c_loaded", RING_Y)
        mask_loaded = sem("mask_loaded")
        keysD_loaded = sems("keysD_loaded", RING_K)
        out_stored = sems("out_stored", 2)
        small = sem("small")
        setup_done = sem("setup_done")
        c_ready = sem("c_ready")
        c_out = sem("c_out")
        wM_built = sems("wM_built", RING)
        wM_scaled = sems("wM_scaled", RING)
        x1_done = sems("x1_done", RING)
        main_out = sems("main_out", 2)
        rest_out = sems("rest_out", 2)
        st_main_done = sems("st_main_done", RING)
        st_rest_done = sems("st_rest_done", 2)
        stat_in = sem("stat_in")
        stat_sum = sem("stat_sum")
        root_in = sem("root_in")
        root_out = sem("root_out")
        dice_ready = sem("dice_ready")
        p1_ready = sems("p1_ready", RING)
        h1_ready = sems("h1_ready", RING)
        y1_ready = sems("y1_ready", RING)
        x2_done = sems("x2_done", RING)
        x2_out = sems("x2_out", RING)
        st2_done = sems("st2_done", RING)
        p2_ready = sems("p2_ready", RING_C)
        h2_ready = sems("h2_ready", RING_Y)
        y2_ready = sems("y2_ready", RING_Y)
        pool_c = sem("pool_c")
        mask_ready = sem("mask_ready")
        xm_ready = sem("xm_ready")
        x3_done = sems("x3_done", RING_C)
        x3_out = sem("x3_out")
        st3_done = sem("st3_done")
        p3_ready = sem("p3_ready")
        s_ready = sem("s_ready")
        sT_done = sem("sT_done")
        sT_out = sems("sT_out", 2)
        sU_ready = sems("sU_ready", RING_D)
        o_done = sems("o_done", RING_D)
        o_out = sems("o_out", RING_D)

        def wait_reuse(eng, s, n):
            if not (isinstance(n, int) and n == 0):
                eng.wait_ge(s, n)

        block = ctx.enter_context(nc.Block())

        @block.sync
        def _(sp):
            w1_v = w1.rearrange("(i e) c -> e i c", i=4)
            for h in range(2):
                sp.dma_start(w1s[64 * h:64 * h + 64, :, :], w1_v).then_inc(w1_loaded, 16)
            sp.dma_start(par[:, :], params).then_inc(w1_loaded, 16)
            sp.dma_start(qT, queriesT).then_inc(w1_loaded, 16)

            def load_keys(i, r):
                sp.dma_start(keysA[:, r, :], keysT[bass.ds(RING * i + r, 1), :, :]
                             .rearrange("a p n -> (a p) n")).then_inc(keysA_loaded[r], 16)

            def store_x1(i, r):
                sp.wait_ge(main_out[r % 2], 2 * i + (r // 2 + 1))
                sp.dma_start(x1_main[bass.ds(RING * i + r, 1), :, :].rearrange("a p n -> (a p) n"),
                             xMain[:, r, :]).then_inc(x1main_stored[r], 16)
                if r % 2:
                    b = r // 2
                    sp.wait_ge(rest_out[b], i + 1)
                    sp.dma_start(x1_rest[bass.ds(2 * i + b, 1), :, :].rearrange("a p n -> (a p) n"),
                                 xRest[:, b, :]).then_inc(x1rest_stored[b], 16)

            for r in range(RING):
                load_keys(0, r)
            sp.dma_start(con[:, :], consts).then_inc(con_loaded, 16)
            with sp.Fori(1, BLOCKS) as i:
                for r in range(RING):
                    sp.wait_ge(x1_done[r], i)
                    load_keys(i, r)
                    store_x1(i - 1, r)
            for r in range(RING):
                store_x1(BLOCKS - 1, r)

            for r in range(RING):
                sp.wait_ge(x1main_stored[r], 16 * BLOCKS)
            for b in range(2):
                sp.wait_ge(x1rest_stored[b], 16 * BLOCKS)

            for r in range(RING):
                sp.wait_ge(st_main_done[r], BLOCKS)
            for b in range(2):
                sp.wait_ge(st_rest_done[b], BLOCKS)

            def load_x1(i, r):
                sp.dma_start(x1[0:MAIN, r, :].rearrange("c (h n) -> c h n", h=2),
                             x1_main[bass.ds(RING_X * i + r, 1), :, :]
                             .rearrange("a (h c) n -> (a c) h n", h=2)).then_inc(x1_loaded[r], 16)
                g = r % 2
                rest = x1_rest[bass.ds(RING_X // 2 * i + r // 2, 1), :, g * TOKENS:(g + 1) * TOKENS]
                for h in range(2):
                    sp.dma_start(x1[MAIN:H1, r, h * COLS:(h + 1) * COLS].rearrange("c (j t) -> c j t", j=4),
                                 rest.rearrange("a (j h c) t -> h (a c) j t", j=4, h=2)[h]
                                 ).then_inc(x1_loaded[r], 16)

            def blocks_b(i):
                for r in range(RING_X):
                    sp.wait_ge(x2_done[r % RING], 2 * (i - 1) + (r // RING + 1))
                    load_x1(i, r)

            for r in range(RING_X):
                load_x1(0, r)
            with sp.Fori(1, BLOCKS_X) as i:
                blocks_b(i)

            for b in range(PAIRS):
                sp.wait_ge(x2_stored[b], 32 * BLOCKS_X)
            for r in range(RING):
                sp.wait_ge(st2_done[r], BLOCKS)

            def load_x2(F, t):
                q = t % RING_Y
                if not (isinstance(F, int) and F == 0 and t < RING_Y):
                    use = (FULL // RING_Y) * F + t // RING_Y
                    sp.wait_ge(h2_ready[q], use)
                    sp.wait_ge(y2_ready[q], use)
                sp.dma_start(x2c[0:2 * H2, q, :, :],
                             x2_dram[bass.ds(2 * (FULL * F + t), 2), :, :].rearrange("g c n -> c g n")
                             ).then_inc(x2c_loaded[q], 16)

            def load_unit(i, r):
                for c, n in enumerate(CHUNKS):
                    sp.dma_start(keysD[r][0:n, c, :, :],
                                 keysU[bass.ds(RING_K * i + r, 1), c * CHUNKS[0]:c * CHUNKS[0] + n, :, :]
                                 .rearrange("a p t n -> (a p) t n")).then_inc(keysD_loaded[r], 16)

            for F in range(4):
                for t in range(FULL):
                    load_x2(F, t)
                    if F == 0 and t == RING_Y - 1:
                        sp.dma_start(maskI, mask).then_inc(mask_loaded, 16)
                    if t == FULL * 3 // 4:
                        load_unit(0, F)
            with sp.Fori(4, FULLS) as F:
                for t in range(FULL):
                    load_x2(F, t)

            def store_out(i, s):
                for b in range(8):
                    sp.dma_start(out[bass.ds(RING_D * i, RING_D), :, b, :].rearrange("u t e -> t u e"),
                                 oD[b:b + 97:32, s, :, E * b:E * b + E]).then_inc(out_stored[s], 16)

            def sums_stored(i, s):
                for q in range(RING_D):
                    sp.wait_ge(o_out[q], 2 * i + (s + 1))
                store_out(2 * i + s, s)

            for n, q in ((4, RING_Y - 3), (5, RING_Y - 1), (6, RING_Y - 1), (7, RING_Y - 1)):
                sp.wait_ge(x3_done[q % RING_C], TILES_C // RING_C)
                load_unit(0, n)
            with sp.Fori(1, BLOCKS_D) as i:
                for r in range(RING_K):
                    sp.wait_ge(o_done[r % RING_D], 2 * (i - 1) + (r // RING_D + 1))
                    load_unit(i, r)
                    if r % RING_D == RING_D - 1:
                        sums_stored(i - 1, r // RING_D)
            for s in range(2):
                sums_stored(BLOCKS_D - 1, s)
            for s in range(2):
                sp.wait_ge(out_stored[s], 16 * 8 * BLOCKS_D)

        @block.gpsimd
        def _(pool):
            pool.wait_ge(setup_done, 1)

            def add_wB(i, r):
                pool.wait_ge(wM_scaled[r], i + 1)
                pool.tensor_tensor(wM[:, r, :, :], wM[:, r, :, :],
                                   wB[:, :].unsqueeze(1).broadcast_to([P, 4, MCOLS]),
                                   ALU.add).then_inc(wM_built[r], 1)

            with pool.Fori(0, BLOCKS) as i:
                for r in range(RING):
                    add_wB(i, r)

            def gate1_pool(i, r):
                pool.wait_ge(p1_ready[r % RING], 2 * i + (r // RING + 1))
                y = h1[0:H1, r, :].rearrange("p (h n) -> p h n", h=2)[:, :, CUT_B:]
                pool.tensor_tensor(y, y, x1[0:H1, r, :].rearrange("p (h n) -> p h n", h=2)[:, :, CUT_B:],
                                   ALU.mult).then_inc(y1_ready[r % RING], 1)

            with pool.Fori(0, BLOCKS_X) as i:
                for r in range(RING_X):
                    gate1_pool(i, r)

            beta2 = beta[0:2 * H2, 1:2].broadcast_to([2 * H2, POOL_C])

            def unmask(F):
                n = bass.ds(2 * TOKENS * F, 2 * TOKENS)
                pool.wait_ge(x3_out, F + 1)
                pool.tensor_tensor(maskF[:, n], maskF[:, n], x3[:, n], ALU.mult).then_inc(xm_ready, 1)

            def gate2_pool(F):
                for t in range(FULL):
                    q = t % RING_C
                    pool.wait_ge(p2_ready[q], (FULL // RING_C) * F + (t // RING_C + 1))
                    y = p2[0:2 * H2, q, CUT_C:]
                    pool.tensor_tensor(y, y, beta2, ALU.add).then_inc(pool_c, 1)
                    pool.wait_ge(pool_c, FULL * F + (t + 1))
                    pool.tensor_tensor(y, y, x2c[0:2 * H2, t % RING_Y, 1, CUT_C - COLS:], ALU.mult
                                       ).then_inc(y2_ready[t % RING_Y], 1)
                    if t == FULL // 2 and not (isinstance(F, int) and F == 0):
                        unmask(F - 1)

            gate2_pool(0)
            pool.wait_ge(mask_loaded, 16)
            pool.tensor_scalar(maskF, maskI, -1.0, 1.0, ALU.mult, ALU.add).then_inc(mask_ready, 1)
            pool.wait_ge(mask_ready, 1)
            with pool.Fori(1, FULLS) as F:
                gate2_pool(F)
            unmask(FULLS - 1)

        @block.tensor
        def _(pe):
            pe.wait_ge(setup_done, 1)
            half = GROUPS * 2
            for n in range(2):
                for h in range(2):
                    rows = slice(64 * h, 64 * h + 64)
                    pe.matmul(psum[rows, 6 + n, 0:half], wA[rows, 0:MAIN], qT[rows, n * half:(n + 1) * half],
                              start=True, stop=True)
            qj = qT.rearrange("p (g j) -> p j g", j=4)
            for j in range(4):
                last = pe.matmul(psum[32 * j:32 * j + 32, 5, 0:GROUPS], wArest[:, :], qj[:, j, :],
                                 start=True, stop=True)
            last.then_inc(c_ready, 1)

            def x1_group(i, r):
                s, b = r % 2, r // 2
                pe.wait_ge(keysA_loaded[r], 16 * i + 16)
                wait_reuse(pe, main_out[s], 2 * i + r // 2)
                if s == 0:
                    wait_reuse(pe, rest_out[b], i)
                pe.wait_ge(wM_built[r], i + 1)
                for j in range(4):
                    c = (j % 2) * TOKENS
                    pe.matmul(psum[:, 2 * s + j // 2, c:c + TOKENS], wM[:, r, j, 0:2 * MAIN],
                              keysA[:, r, j * TOKENS:(j + 1) * TOKENS], start=True, stop=True)
                for j in range(4):
                    last = pe.matmul(psum[32 * j:32 * j + 32, 4 + b, s * TOKENS:(s + 1) * TOKENS],
                                     wM[:, r, j, 2 * MAIN:MCOLS], keysA[:, r, j * TOKENS:(j + 1) * TOKENS],
                                     start=True, stop=True)
                last.then_inc(x1_done[r], 1)

            for r in range(RING):
                if r == 2:
                    pe.wait_ge(c_out, 1)
                x1_group(0, r)
            with pe.Fori(1, BLOCKS) as i:
                for r in range(RING):
                    x1_group(i, r)

            def averages(step, rows, outs):
                pe.wait_ge(stat_in, step)
                for at, m, terms in outs:
                    for n, (k, v) in enumerate(terms):
                        last = pe.matmul(psum[0:m, 6, at:at + 1], con[0:rows, k:k + m], tmp[0:rows, v:v + 1],
                                         start=(n == 0), stop=(n == len(terms) - 1))
                last.then_inc(stat_sum, 1)

            def warm_up():
                for _ in range(4):
                    pe.matmul(psum[:, 7, :], con[:, 0:P], con[:, 0:BANK], start=True, stop=True)

            averages(1, P, [(0, P, ((K_GA, 0),)), (1, P, ((K_GB, 2),))])
            averages(2, P, [(2, H1, ((K_SA, 0), (K_SB, 2))), (3, H1, ((K_SA, T_SPREAD), (K_SB, T_SPREAD + 1)))])

            warm_up()
            pe.wait_ge(dice_ready, 1)

            def x2_group(i, r):
                q = r % RING
                wait_reuse(pe, x2_out[q], 2 * i + r // RING)
                pe.wait_ge(h1_ready[q], 2 * i + (r // RING + 1))
                x = (h1[0:H1, r, :], x1[0:H1, r, :])
                for a in range(2):
                    if a == 1:
                        pe.wait_ge(y1_ready[q], 2 * i + (r // RING + 1))
                    for h in range(2):
                        c = h * COLS + a * (COLS // 2)
                        pe.matmul(psum[64 * h:64 * h + 64, 2 * q + a, 0:COLS // 2], w2d[0:H1, :],
                                  x[0][:, c:c + COLS // 2], start=True, stop=(a == 0))
                for h in range(2):
                    last = pe.matmul(psum[64 * h:64 * h + 64, 2 * q + 1, COLS // 2 - POOL_B:COLS // 2],
                                     w2a[0:H1, :], x[1][:, h * COLS + CUT_B:(h + 1) * COLS],
                                     start=False, stop=True)
                last.then_inc(x2_done[q], 1)

            for r in range(RING_X):
                x2_group(0, r)
            with pe.Fori(1, BLOCKS_X) as i:
                for r in range(RING_X):
                    x2_group(i, r)

            averages(3, P, [(0, P, ((K_G2, 0),))])
            averages(4, P, [(2, 2 * H2, ((K_S2, 0),)), (3, 2 * H2, ((K_S2, T_SPREAD),))])

            warm_up()
            pe.wait_ge(dice_ready, 2)

            def x3_bank(F, bank):
                if not (isinstance(F, int) and F < 2):
                    pe.wait_ge(x3_out, F - 1)
                for t in range(FULL):
                    q = t % RING_C
                    use = (FULL // RING_Y) * F + (t // RING_Y + 1)
                    pe.wait_ge(h2_ready[t % RING_Y], use)
                    for g in range(2):
                        for a in range(2):
                            ct = 2 * g + a
                            c = g * COLS + a * 2 * TOKENS
                            if ct == 3:
                                pe.wait_ge(y2_ready[t % RING_Y], use)
                            last = pe.matmul(psum[32 * ct:32 * ct + 32, bank, 0:2 * TOKENS],
                                             w3z[0:2 * H2, 30 - 2 * t:62 - 2 * t],
                                             p2[0:2 * H2, q, c:c + 2 * TOKENS],
                                             start=(t == 0), stop=(t == FULL - 1))
                    last.then_inc(x3_done[q], 1)

            for bank in range(2):
                x3_bank(bank, bank)
            with pe.Fori(1, FULLS // 2) as F2:
                for bank in range(2):
                    x3_bank(2 * F2 + bank, bank)

            averages(5, P, [(0, P, ((K_G3, 0),))])
            averages(6, P, [(2, P, ((K_G3, 0),)), (3, P, ((K_G3, T_SPREAD),))])

            def turn(n):
                pe.wait_ge(s_ready, n + 1)
                if n >= 2:
                    pe.wait_ge(sT_out[0], n)
                    pe.wait_ge(sT_out[1], n - 1)
                for par_ in range(2):
                    c0 = (2 * n + par_) * TOKENS
                    for c, m in enumerate(CHUNKS):
                        last = pe.transpose(psum[0:m, c + 2 * (n % 2), par_ * P:(par_ + 1) * P],
                                            s3[:, c0:c0 + m], con[:, K_ID:K_ID + P])
                        c0 += m
                last.then_inc(sT_done, 1)

            def unit_sums(i, r):
                q = r % RING_D
                pe.wait_ge(keysD_loaded[r], 32 * i + 32)
                wait_reuse(pe, o_out[q], 2 * i + r // RING_D)
                pe.wait_ge(sU_ready[q], 2 * i + (r // RING_D + 1))
                for c, n in enumerate(CHUNKS):
                    for t in range(4):
                        last = pe.matmul(psum[32 * t:32 * t + 32, 4 + q, :], sU[0:n, q, c, 8 * t:8 * t + 32],
                                         keysD[r][0:n, c, t, :], start=(c == 0), stop=(c == 1))
                last.then_inc(o_done[q], 1)

            for n in range(2):
                turn(n)
            for r in range(RING_D):
                unit_sums(0, r)
            for n in range(2, FULLS):
                turn(n)
            for r in range(RING_D, RING_K):
                unit_sums(0, r)
            with pe.Fori(1, BLOCKS_D) as i:
                for r in range(RING_K):
                    unit_sums(i, r)

        @block.scalar
        def _(act):
            def root(n, rows=P):
                act.wait_ge(root_in, n)
                act.activation(tmp[0:rows, T_ROOT:T_ROOT + 1], tmp[0:rows, T_VAR:T_VAR + 1], ACT.Sqrt
                               ).then_inc(root_out, 1)

            def scale_wD(i, r):
                wait_reuse(act, x1_done[r], i)
                act.wait_ge(setup_done, 1)
                for j in range(4):
                    last = act.activation(wM[:, r, j, :], wD[:, :], ACT.Identity, bias=0.0,
                                          scale=qT[:, bass.ds(4 * RING * i + 4 * r + j, 1)])
                last.then_inc(wM_scaled[r], 1)

            for r in range(RING):
                scale_wD(0, r)
            with act.Fori(1, BLOCKS) as i:
                for r in range(RING):
                    scale_wD(i, r)

            root(1, H1)

            act.wait_ge(dice_ready, 1)

            def sigmoid1(i, r):
                q = r % RING
                act.wait_ge(x1_loaded[r], 48 * i + 48)
                act.activation(h1[0:H1, r, :], x1[0:H1, r, :], ACT.Sigmoid, bias=bias[0:H1, 0:1],
                               scale=scale[0:H1, 0:1]).then_inc(p1_ready[q], 1)

            def x2_from_psum(i, r):
                q = r % RING
                act.wait_ge(x2_done[q], 2 * i + (r // RING + 1))
                if not (isinstance(i, int) and i == 0):
                    act.wait_ge(x2_stored[r // 2], 32 * i)
                    act.wait_ge(st2_done[q], 2 * (i - 1) + (r // RING + 1))
                act.activation(x2[:, r, :].rearrange("p (a n) -> p a n", a=2),
                               psum[:, 2 * q:2 * q + 2, 0:COLS // 2], ACT.Identity,
                               bias=par[:, Q_B2:Q_B2 + 1]).then_inc(x2_out[q], 1)

            def store_x2(i, r):
                b, h = r // 2, r % 2
                for g in (2 * b, 2 * b + 1):
                    act.wait_ge(x2_out[g % RING], 2 * i + (g // RING + 1))
                act.dma_start(x2_dram[bass.ds(RING_X * i + 2 * b, 2), h * H2:(h + 1) * H2, :]
                              .rearrange("g c n -> c g n"),
                              x2[64 * h:64 * h + H2, 2 * b:2 * b + 2, :]).then_inc(x2_stored[b], 16)

            def block_b(i):
                first = isinstance(i, int) and i == 0
                for r in range(RING_X):
                    sigmoid1(i, r)
                    if (r - 3) % RING_X not in BY_V and not (first and r < 3):
                        x2_from_psum(i if r >= 3 else i - 1, (r - 3) % RING_X)
                    if not (first and r < 6):
                        store_x2(i if r >= 6 else i - 1, (r - 6) % RING_X)

            block_b(0)
            block_b(1)
            with act.Fori(2, BLOCKS_X) as i:
                block_b(i)
            for r in (RING_X - 3, RING_X - 2):
                x2_from_psum(BLOCKS_X - 1, r)
            for r in range(2, RING_X):
                store_x2(BLOCKS_X - 1, r)

            root(2, 2 * H2)

            act.wait_ge(dice_ready, 2)

            def sigmoid2(F):
                for t in range(FULL):
                    q = t % RING_C
                    act.wait_ge(x2c_loaded[t % RING_Y], 16 * ((FULL // RING_Y) * F + (t // RING_Y + 1)))
                    wait_reuse(act, x3_done[q], (FULL // RING_C) * F + t // RING_C)
                    act.activation(p2[0:2 * H2, q, :],
                                   x2c[0:2 * H2, t % RING_Y, :, :].rearrange("p g n -> p (g n)"),
                                   ACT.Sigmoid, bias=bias[0:2 * H2, 1:2], scale=scale[0:2 * H2, 1:2]
                                   ).then_inc(p2_ready[q], 1)

            sigmoid2(0)
            with act.Fori(1, FULLS) as F:
                sigmoid2(F)

            root(3)
            act.wait_ge(dice_ready, 3)
            act.wait_ge(mask_ready, 1)
            def sigmoid3(n):
                part = slice(2 * TOKENS * n, 2 * TOKENS * (n + 1))
                act.activation(s3[:, part], x3[:, part], ACT.Sigmoid, bias=bias[:, 2:3], scale=scale[:, 2:3]
                               ).then_inc(p3_ready, 1)

            def turned(n):
                m = CHUNKS[1]
                act.wait_ge(sT_done, n + 1)
                act.copy(sT[0:m, 1, 2 * P * n:2 * P * (n + 1)], psum[0:m, 1 + 2 * (n % 2), 0:2 * P]
                         ).then_inc(sT_out[1], 1)

            def unit_scores(i, r):
                q = r % RING_D
                wait_reuse(act, o_done[q], 2 * i + r // RING_D)
                act.wait_ge(dice_ready, 3)
                for c, n in enumerate(CHUNKS):
                    last = act.copy(sU[0:n, q, c, 0:56], sT[0:n, c, bass.ds(32 * (RING_K * i + r), 56)])
                last.then_inc(sU_ready[q], 1)

            for n in range(4):
                sigmoid3(n)
            for n in range(2):
                turned(n)
            act.wait_ge(sT_out[0], 1 + 2)
            act.wait_ge(sT_out[1], 2)
            for r in range(RING_D):
                unit_scores(0, r)
            for n in range(4, FULLS):
                sigmoid3(n)
            for n in range(2, FULLS):
                turned(n)
            act.wait_ge(sT_out[0], 1 + FULLS)
            act.wait_ge(sT_out[1], FULLS)
            for r in range(RING_D, RING_K):
                unit_scores(0, r)
            with act.Fori(1, BLOCKS_D) as i:
                for r in range(RING_K):
                    unit_scores(i, r)

        @block.vector
        def _(v):
            steps = [0]

            def link(ins):
                steps[0] += 1
                ins.then_inc(small, 1)
                v.wait_ge(small, steps[0])

            def col(k, rows=P):
                return tmp[0:rows, k:k + 1]

            for t in (wB, wD):
                v.memset(t[:, :], 0.0)
            link(v.memset(wArest[:, :], 0.0))
            v.wait_ge(w1_loaded, 64)
            link(v.tensor_tensor(wA[:, :], w1s[:, 0, :], w1s[:, 2, :], ALU.add))
            for h in range(2):
                rows, main, at = slice(64 * h, 64 * h + 64), MAIN * h, REST * h
                v.tensor_copy(wArest[rows, at:at + REST], wA[rows, MAIN:H1])
                for a, b, n in ((main, 0, MAIN), (2 * MAIN + at, MAIN, REST)):
                    v.tensor_tensor(wB[rows, a:a + n], w1s[rows, 1, b:b + n], w1s[rows, 2, b:b + n], ALU.subtract)
                    last = v.tensor_copy(wD[rows, a:a + n], w1s[rows, 3, b:b + n])
            last.then_inc(setup_done, 1)

            v.wait_ge(c_ready, 1)
            v.tensor_scalar(cMain.rearrange("p (a n) -> p a n", a=2), psum[:, 6:8, 0:2 * GROUPS],
                            par[:, Q_B1A:Q_B1A + 1], None, ALU.add)
            v.tensor_scalar(cRest, psum[:, 5, 0:GROUPS], par[:, Q_B1B:Q_B1B + 1], None, ALU.add
                            ).then_inc(c_out, 1)
            v.wait_ge(c_out, 1)

            def dice_constants():
                for t in (w2d, w2a, w3z):
                    v.memset(t[:, :], 0.0)
                link(v.memset(tmp[:, :], 0.0))
                alpha, t3 = par[:, Q_AL:Q_AL + 3], tmp[:, 0:3]
                link(v.tensor_scalar(dd[:, :], alpha, -1.0, 1.0, ALU.mult, ALU.add))
                link(v.tensor_scalar(t3, dd[:, :], 0.0, TINY, ALU.is_equal, ALU.mult))
                link(v.tensor_tensor(dd[:, :], dd[:, :], t3, ALU.add))
                link(v.reciprocal(t3, dd[:, :]))
                link(v.tensor_tensor(beta[:, :], t3, alpha, ALU.mult))
                for w, by in ((w2d, dd[0:H1, 0:1]), (w2a, par[0:H1, Q_AL:Q_AL + 1])):
                    v.tensor_scalar(w[0:H1, 0:H2], par[0:H1, Q_W2:Q_W2 + H2], by, None, ALU.mult)
                link(v.tensor_scalar(w3z[0:2 * H2, 30:32], par[0:2 * H2, Q_W3A:Q_W3A + 2], dd[0:2 * H2, 1:2],
                                     None, ALU.mult))
                v.wait_ge(con_loaded, 16)

            def stats_main(i, r):
                v.wait_ge(main_out[r % 2], 2 * i + (r // 2 + 1))
                for a in range(2):
                    last = v.bn_stats(stMain[:, bass.ds(12 * (RING * i + r) + 6 * a, 6)],
                                      xMain[:, r, a * 2 * TOKENS:(a + 1) * 2 * TOKENS])
                last.then_inc(st_main_done[r], 1)

            def block_a(i):
                for r in range(RING):
                    s, b = r % 2, r // 2
                    wait_reuse(v, x1main_stored[r], 16 * i)
                    wait_reuse(v, st_main_done[r], i)
                    v.wait_ge(x1_done[r], i + 1)
                    c = cMain[:, bass.ds(4 * (RING * i + r), 4)].rearrange("p (a j) -> p a j", a=2)
                    v.tensor_tensor(xMain[:, r, :].rearrange("p (a j t) -> p a j t", a=2, j=2),
                                    psum[:, 2 * s:2 * s + 2, 0:2 * TOKENS].rearrange("p a (j t) -> p a j t", j=2),
                                    c.unsqueeze(3).broadcast_to([P, 2, 2, TOKENS]),
                                    ALU.add).then_inc(main_out[s], 1)
                    if s == 1:
                        wait_reuse(v, x1rest_stored[b], 16 * i)
                        wait_reuse(v, st_rest_done[b], i)
                        c = cRest[:, bass.ds(RING * i + 2 * b, 2)]
                        v.tensor_tensor(xRest[:, b, :].rearrange("p (g t) -> p g t", g=2),
                                        psum[:, 4 + b, 0:2 * TOKENS].rearrange("p (g t) -> p g t", g=2),
                                        c.unsqueeze(2).broadcast_to([P, 2, TOKENS]),
                                        ALU.add).then_inc(rest_out[b], 1)
                    if r:
                        stats_main(i, r - 1)
                stats_main(i, RING - 1)
                for b in range(2):
                    v.wait_ge(rest_out[b], i + 1)
                    v.bn_stats(stRest[:, bass.ds(12 * i + 6 * b, 6)], xRest[:, b, :]
                               ).then_inc(st_rest_done[b], 1)

            block_a(0)
            dice_constants()
            with v.Fori(1, BLOCKS) as i:
                block_a(i)

            def signal(s):
                v.memset(tmp[:, T_NONE:T_NONE + 1], 0.0).then_inc(s, 1)

            def dice(layer, parts, rows):
                means = tmp[:, 0:2 * parts].rearrange("p (w k) -> p k w", k=2)
                dev, spread = tmp[:, T_A:T_A + parts], tmp[:, T_SPREAD:T_SPREAD + parts]
                signal(stat_in)
                v.wait_ge(stat_sum, 2 * layer - 1)
                link(v.tensor_tensor(dev, means[:, 0, :], psum[:, 6, 0:parts], ALU.subtract))
                link(v.tensor_tensor(dev, dev, dev, ALU.mult))
                link(v.tensor_tensor(spread, dev, means[:, 1, :], ALU.add))
                signal(stat_in)
                v.wait_ge(stat_sum, 2 * layer)
                a, var, root, inv = (tmp[0:rows, at:at + 1] for at in (T_A, T_VAR, T_ROOT, T_INV))
                mean = psum[0:rows, 6, 2:3]
                sc, bi = scale[0:rows, layer - 1:layer], bias[0:rows, layer - 1:layer]
                link(v.tensor_scalar(var, psum[0:rows, 6, 3:4], EPS, None, ALU.add))
                signal(root_in)
                v.wait_ge(root_out, layer)
                link(v.reciprocal(inv, root))
                link(v.tensor_tensor(a, inv, inv, ALU.mult))
                link(v.scalar_tensor_tensor(out=a, in0=a, scalar=-0.5, in1=var, op0=ALU.mult, op1=ALU.mult))
                link(v.scalar_tensor_tensor(out=a, in0=a, scalar=1.5, in1=inv, op0=ALU.add, op1=ALU.mult))
                link(v.tensor_tensor(sc, a, par[0:rows, Q_G + layer - 1:Q_G + layer], ALU.mult))
                link(v.tensor_tensor(a, mean, sc, ALU.mult))
                link(v.tensor_tensor(bi, par[0:rows, Q_BE + layer - 1:Q_BE + layer], a, ALU.subtract))
                signal(dice_ready)

            for r in range(RING):
                v.wait_ge(st_main_done[r], BLOCKS)
            for b in range(2):
                v.wait_ge(st_rest_done[b], BLOCKS)
            link(v.bn_aggr(tmp[:, 0:2], stMain))
            link(v.bn_aggr(tmp[:, 2:4], stRest))
            dice(1, 2, H1)

            def gate1(i, r):
                q = r % RING
                v.wait_ge(p1_ready[q], 2 * i + (r // RING + 1))
                p = h1[0:H1, r, :].rearrange("p (h n) -> p h n", h=2)[:, :, 0:CUT_B]
                x = x1[0:H1, r, :].rearrange("p (h n) -> p h n", h=2)[:, :, 0:CUT_B]
                v.scalar_tensor_tensor(out=p, in0=p, scalar=beta[0:H1, 0:1], in1=x, op0=ALU.add, op1=ALU.mult
                                       ).then_inc(h1_ready[q], 1)

            def x2_by_v(i, r):
                q = r % RING
                v.wait_ge(x2_done[q], 2 * i + (r // RING + 1))
                if not (isinstance(i, int) and i == 0):
                    v.wait_ge(x2_stored[r // 2], 32 * i)
                    v.wait_ge(st2_done[q], 2 * (i - 1) + (r // RING + 1))
                v.tensor_scalar(x2[:, r, :].rearrange("p (a n) -> p a n", a=2),
                                psum[:, 2 * q:2 * q + 2, 0:COLS // 2], par[:, Q_B2:Q_B2 + 1], None, ALU.add
                                ).then_inc(x2_out[q], 1)

            def stats_x2(i, r):
                q = r % RING
                v.wait_ge(x2_out[q], 2 * i + (r // RING + 1))
                for a in range(2):
                    last = v.bn_stats(st2[:, bass.ds(12 * (RING_X * i + r) + 6 * a, 6)],
                                      x2[:, r, a * 2 * TOKENS:(a + 1) * 2 * TOKENS])
                last.then_inc(st2_done[q], 1)

            def block_b(i):
                for r in range(RING_X):
                    gate1(i, r)
                    for back, step in ((2, x2_by_v), (3, stats_x2)):
                        before = (r - back) % RING_X
                        if step is x2_by_v and before not in BY_V:
                            continue
                        if r >= back:
                            step(i, before)
                        elif not (isinstance(i, int) and i == 0):
                            step(i - 1, before)

            block_b(0)
            block_b(1)
            with v.Fori(2, BLOCKS_X) as i:
                block_b(i)
            x2_by_v(BLOCKS_X - 1, RING_X - 1)
            for r in (RING_X - 3, RING_X - 2, RING_X - 1):
                stats_x2(BLOCKS_X - 1, r)

            for r in range(RING):
                v.wait_ge(st2_done[r], BLOCKS)
            link(v.bn_aggr(tmp[:, 0:2], st2))
            dice(2, 1, 2 * H2)

            def stats_x3(F):
                v.wait_ge(x3_out, F + 1)
                v.bn_stats(st3[:, bass.ds(6 * F, 6)], x3[:, bass.ds(2 * TOKENS * F, 2 * TOKENS)]
                           ).then_inc(st3_done, 1)

            def x3_from_psum(F, bank):
                v.wait_ge(x3_done[RING_C - 1], (FULL // RING_C) * (F + 1))
                v.tensor_scalar(x3[:, bass.ds(2 * TOKENS * F, 2 * TOKENS)], psum[:, bank, 0:2 * TOKENS],
                                par[:, Q_B3:Q_B3 + 1], None, ALU.add).then_inc(x3_out, 1)

            def gate2(F, bank):
                for t in range(FULL):
                    q = t % RING_C
                    v.wait_ge(p2_ready[q], (FULL // RING_C) * F + (t // RING_C + 1))
                    p = p2[0:2 * H2, q, 0:CUT_C]
                    x = x2c[0:2 * H2, t % RING_Y, :, :].rearrange("p g n -> p (g n)")[:, 0:CUT_C]
                    v.scalar_tensor_tensor(out=p, in0=p, scalar=beta[0:2 * H2, 1:2], in1=x,
                                           op0=ALU.add, op1=ALU.mult).then_inc(h2_ready[t % RING_Y], 1)
                    if not (isinstance(F, int) and F == 0):
                        if t == 2:
                            x3_from_psum(F - 1, 1 - bank)
                        if t == 4:
                            stats_x3(F - 1)

            for bank in range(2):
                gate2(bank, bank)
            with v.Fori(1, FULLS // 2) as F2:
                for bank in range(2):
                    gate2(2 * F2 + bank, bank)
            x3_from_psum(FULLS - 1, 1)
            stats_x3(FULLS - 1)

            v.wait_ge(st3_done, FULLS)
            link(v.bn_aggr(tmp[:, 0:2], st3[:, :]))
            dice(3, 1, P)
            def scores(n):
                part = slice(2 * TOKENS * n, 2 * TOKENS * (n + 1))
                v.wait_ge(p3_ready, n + 1)
                v.wait_ge(xm_ready, n + 1)
                v.scalar_tensor_tensor(out=s3[:, part], in0=s3[:, part], scalar=beta[:, 2:3], in1=maskF[:, part],
                                       op0=ALU.add, op1=ALU.mult).then_inc(s_ready, 1)

            def turned(n):
                m = CHUNKS[0]
                v.wait_ge(sT_done, n + 1)
                v.tensor_copy(sT[0:m, 0, 2 * P * n:2 * P * (n + 1)], psum[0:m, 2 * (n % 2), 0:2 * P]
                              ).then_inc(sT_out[0], 1)

            v.memset(sT[:, :, BATCHES:BATCHES + 32], 0.0).then_inc(sT_out[0], 1)
            for n in range(2):
                scores(n)
            for n in range(2):
                turned(n)
            for n in range(2, FULLS):
                scores(n)

            def sums_out(i2, s):
                for r in range(RING_D):
                    if r == 0:
                        wait_reuse(v, out_stored[s], 16 * 8 * i2)
                    v.wait_ge(o_done[r], 2 * i2 + (s + 1))
                    v.tensor_scalar(oD[:, s, r, :], psum[:, 4 + r, :], dd[:, 2:3], None, ALU.mult
                                    ).then_inc(o_out[r], 1)

            for s in range(2):
                sums_out(0, s)
                if s == 0:
                    for n in range(2, FULLS):
                        turned(n)
            with v.Fori(1, BLOCKS_D) as i2:
                for s in range(2):
                    sums_out(i2, s)


def kernel(**inputs):
    import numpy as np
    import concourse.bacc as bacc
    from concourse.bass_utils import run_bass_kernel_spmd as run

    f32 = np.float32
    a = {k: np.asarray(v) for k, v in inputs.items()}
    w = {k[len("L0_rec_"):]: v for k, v in a.items() if k.startswith("L0_rec_")}
    keys, queries, mask = a["r_keys"], a["r_queries"], a["r_mask"]

    keysT = np.ascontiguousarray(keys.reshape(GROUPS, 2, 4, TOKENS, E).transpose(0, 1, 4, 2, 3)
                                 ).reshape(GROUPS, P, COLS)
    queriesT = np.ascontiguousarray(queries.reshape(GROUPS, 2, 4, E).transpose(1, 3, 0, 2)).reshape(P, 4 * GROUPS)
    order = (8, 16, 2, 2, 2, 2)
    keysU = np.ascontiguousarray(
        keys.reshape(*order, TOKENS, E).transpose(0, 5, 2, 4, 1, 3, 6, 7)
        .reshape(UNITS, 4, 8, TOKENS, E).transpose(0, 3, 1, 2, 4)).reshape(UNITS, TOKENS, 4, BANK)
    maskU = np.ascontiguousarray(mask.reshape(*order, TOKENS).transpose(2, 4, 1, 3, 0, 5, 6)
                                 ).reshape(P, FULLS * 2 * TOKENS)

    par = np.zeros((P, Q_COLS), f32)
    for at, name in ((Q_G, "g"), (Q_BE, "be"), (Q_AL, "alpha")):
        par[:H1, at] = w[name + "1"]
        par[:2 * H2, at + 1] = np.tile(w[name + "2"], 2)
        par[:, at + 2] = np.tile(w[name + "3"], P)
    par[:, Q_B1A], par[:, Q_B1B] = np.tile(w["b1"][:MAIN], 2), np.tile(w["b1"][MAIN:], 8)
    par[:, Q_B3] = np.tile(w["b3"], P)
    for h in range(2):
        par[64 * h:64 * h + H2, Q_B2] = w["b2"]
        par[H2 * h:H2 * h + H2, Q_W3A + h] = w["W3"][:, 0]
    par[:H1, Q_W2:] = w["W2"]

    con = np.zeros((P, K_COLS), f32)
    p = np.arange(P)
    chA, chB = p % MAIN, MAIN + p % REST
    ch2 = np.where(p % 64 < H2, p % 64, -1 - p)
    con[:, K_ID:K_ID + P] = np.eye(P)
    con[:, K_GA:K_GA + P] = (chA[:, None] == chA) / 2
    con[:, K_GB:K_GB + P] = (chB[:, None] == chB) / 8
    con[:, K_SA:K_SA + H1] = (chA[:, None] == np.arange(H1)) / 2
    con[:, K_SB:K_SB + H1] = (chB[:, None] == np.arange(H1)) / 8
    con[:, K_G2:K_G2 + P] = (ch2[:, None] == ch2) / 2
    con[:, K_S2:K_S2 + 2 * H2] = (ch2[:, None] == np.arange(2 * H2) % H2) / 2
    con[:, K_G3:K_G3 + P] = 1 / P

    nc = bacc.Bacc("TRN2", target_bir_lowering=False, num_devices=1)
    arrays, args = {}, []
    for name, x in (("keysT", keysT), ("keysU", keysU), ("queriesT", queriesT), ("mask", maskU),
                    ("w1", w["W1"]), ("params", par), ("consts", con)):
        arrays[name] = np.ascontiguousarray(x)
        args.append(nc.dram_tensor(name, x.shape, mybir.dt.from_np(x.dtype), kind="ExternalInput").ap())
    args.append(nc.dram_tensor("x1_main", (GROUPS, P, COLS), F32, kind="Internal").ap())
    args.append(nc.dram_tensor("x1_rest", (GROUPS // 2, P, 2 * TOKENS), F32, kind="Internal").ap())
    args.append(nc.dram_tensor("x2_dram", (GROUPS, 2 * H2, COLS), F32, kind="Internal").ap())
    args.append(nc.dram_tensor("out", (UNITS, 4, 8, E), F32, kind="ExternalOutput").ap())
    mask_dice_attention(nc, *args)
    got = run(nc, [arrays], core_ids=[0]).results[0]["out"]
    return np.ascontiguousarray(got.reshape(8, 2, 2, 2, 16, 2, E).transpose(0, 4, 2, 5, 3, 1, 6)
                                ).reshape(BATCHES, 1, E)
```
